# Optimizing a Trainium2 kernel written in Bass

```python
import numpy as np
import jax
import jax.numpy as jnp

def _softmax(x, axis=-1):
    return jax.nn.softmax(x, axis=axis)

def _gelu(x):
    return jax.nn.gelu(x, approximate=True)

def _silu(x):
    return jax.nn.silu(x)

def _sigmoid(x):
    return jax.nn.sigmoid(x)

def _layernorm(x, axis=-1, eps=1e-05):
    m = jnp.mean(x, axis=axis, keepdims=True)
    v = jnp.var(x, axis=axis, keepdims=True)
    return (x - m) / jnp.sqrt(v + eps)

def _scatter_add(tgt, idx, src, axis=0):
    return tgt.at[idx].add(src)

def _segment_sum(src, seg, n):
    return jax.ops.segment_sum(src, seg, n)
kernel_name = 'mk_sandwich_d1_jaxref_r4_cc52a4'

def setup_inputs(seed: int=0):
    np.random.seed(seed)
    _w = jnp.asarray

    def _L0_attn_setup():
        import jax, jax.numpy as jnp
        import numpy as np
        import math
        D_MODEL = 256
        NUM_HEADS = 16
        key = jax.random.key(seed)
        k1, k2, k3 = jax.random.split(key, 3)
        B, S = (2, 512)
        x = jax.random.normal(k1, (B, S, D_MODEL), dtype=jnp.float32)
        W_kqv = jax.random.normal(k2, (D_MODEL, 3 * D_MODEL), dtype=jnp.float32) * (1.0 / math.sqrt(D_MODEL))
        m = jax.random.normal(k3, (NUM_HEADS, 1, 1), dtype=jnp.float32)
        return {'x': x, 'W_kqv': W_kqv, 'm': m}
    _L0_attn_in = _L0_attn_setup()

    def _L0_ffn_setup():
        import jax, jax.numpy as jnp
        import numpy as np
        D_IN, D_HID = (256, 1024)

        def _ternary(key, shape):
            return jax.random.randint(key, shape, -1, 2).astype(jnp.float32)

        def _tlin(x, w, s):
            return jnp.einsum('bsi,oi->bso', x, w) * s
        key = jax.random.key(seed)
        ks = jax.random.split(key, 12)
        inv = lambda fan: 1.0 / np.sqrt(fan).astype(np.float32)
        return {'x': jax.random.normal(ks[0], (4, 512, D_IN), dtype=jnp.float32), 'w1_w': _ternary(ks[1], (D_HID, D_IN)), 'w1_s': jax.random.uniform(ks[2], (D_HID,), dtype=jnp.float32) * inv(D_IN), 'w2_w': _ternary(ks[3], (D_HID, D_IN)), 'w2_s': jax.random.uniform(ks[4], (D_HID,), dtype=jnp.float32) * inv(D_IN), 'h1_w': _ternary(ks[5], (D_HID, D_HID)), 'h1_s': jax.random.uniform(ks[6], (D_HID,), dtype=jnp.float32) * inv(D_HID), 'h2_w': _ternary(ks[7], (D_HID, D_HID)), 'h2_s': jax.random.uniform(ks[8], (D_HID,), dtype=jnp.float32) * inv(D_HID), 'w3_w': _ternary(ks[9], (D_IN, D_HID)), 'w3_s': jax.random.uniform(ks[10], (D_IN,), dtype=jnp.float32) * inv(D_HID)}
    _L0_ffn_in = _L0_ffn_setup()
    _d = {'L0_attn_x': _L0_attn_in['x'], 'L0_attn_W_kqv': _L0_attn_in['W_kqv'], 'L0_attn_m': _L0_attn_in['m'], 'L0_ffn_w1_w': _L0_ffn_in['w1_w'], 'L0_ffn_w1_s': _L0_ffn_in['w1_s'], 'L0_ffn_w2_w': _L0_ffn_in['w2_w'], 'L0_ffn_w2_s': _L0_ffn_in['w2_s'], 'L0_ffn_h1_w': _L0_ffn_in['h1_w'], 'L0_ffn_h1_s': _L0_ffn_in['h1_s'], 'L0_ffn_h2_w': _L0_ffn_in['h2_w'], 'L0_ffn_h2_s': _L0_ffn_in['h2_s'], 'L0_ffn_w3_w': _L0_ffn_in['w3_w'], 'L0_ffn_w3_s': _L0_ffn_in['w3_s']}
    _x0 = _d['L0_attn_x']
    _d['L0_attn_x'] = jax.random.normal(jax.random.fold_in(jax.random.key(seed), 1), (2, 2048, 256), dtype=_x0.dtype)
    del _x0
    return _d

def reference(L0_attn_x, L0_attn_W_kqv, L0_attn_m, L0_ffn_w1_w, L0_ffn_w1_s, L0_ffn_w2_w, L0_ffn_w2_s, L0_ffn_h1_w, L0_ffn_h1_s, L0_ffn_h2_w, L0_ffn_h2_s, L0_ffn_w3_w, L0_ffn_w3_s):

    def _L0_attn_ref(x, W_kqv, m):
        import jax, jax.numpy as jnp
        import numpy as np
        import math
        D_MODEL = 256
        NUM_HEADS = 16
        B, S, D = x.shape
        H = NUM_HEADS
        hd = D // H
        scale = math.sqrt(D)
        kqv = x @ W_kqv
        k, q, v = jnp.split(kqv, 3, axis=-1)
        q = q.reshape(B, S, H, hd)
        k = k.reshape(B, S, H, hd)
        v = v.reshape(B, S, H, hd)
        rel = (jnp.arange(S)[None, :] - jnp.arange(S)[:, None]).astype(x.dtype)
        bias = m[None, :, :, :] * rel[None, None, :, :]
        score = jnp.einsum('bqhd,bkhd->bhqk', q, k) / scale + bias
        causal = jnp.tril(jnp.ones((S, S), dtype=bool))
        score = jnp.where(causal[None, None, :, :], score, -jnp.inf)
        attn = jax.nn.softmax(score, axis=-1)
        out = jnp.einsum('bhqk,bkhd->bqhd', attn, v).reshape(B, S, D)
        return out

    def _L0_ffn_ref(x, w1_w, w1_s, w2_w, w2_s, h1_w, h1_s, h2_w, h2_s, w3_w, w3_s):
        import jax, jax.numpy as jnp
        import numpy as np
        D_IN, D_HID = (256, 1024)

        def _ternary(key, shape):
            return jax.random.randint(key, shape, -1, 2).astype(jnp.float32)

        def _tlin(x, w, s):
            return jnp.einsum('bsi,oi->bso', x, w) * s
        h = jax.nn.silu(_tlin(x, w1_w, w1_s)) * _tlin(x, w2_w, w2_s)
        h = jax.nn.gelu(_tlin(h, h1_w, h1_s), approximate=False)
        h = jax.nn.gelu(_tlin(h, h2_w, h2_s), approximate=False)
        return _tlin(h, w3_w, w3_s)
    x = L0_attn_x
    x = x + _layernorm(_L0_attn_ref(_layernorm(x, axis=-1), L0_attn_W_kqv, L0_attn_m), axis=-1)
    x = x + _layernorm(_L0_ffn_ref(_layernorm(x, axis=-1), L0_ffn_w1_w, L0_ffn_w1_s, L0_ffn_w2_w, L0_ffn_w2_s, L0_ffn_h1_w, L0_ffn_h1_s, L0_ffn_h2_w, L0_ffn_h2_s, L0_ffn_w3_w, L0_ffn_w3_s), axis=-1)
    return x

_drawn_inputs = setup_inputs


def setup_inputs(seed=0):
    import zlib

    import numpy as np

    out = dict(_drawn_inputs(seed))
    spreads = {}
    factors = {}
    for name, (base, spread) in spreads.items():
        noise = np.random.default_rng([zlib.crc32(name.encode()), seed]).standard_normal(out[name].shape)
        drawn = base * np.exp(spread * noise) if base else spread * noise
        out[name] = jnp.asarray(drawn.astype(out[name].dtype))
    for name, factor in factors.items():
        out[name] = (out[name] * factor).astype(out[name].dtype)
    return out
```

```python
import concourse.bass as bass
from concourse import mybir
from contextlib import ExitStack

F32 = mybir.dt.float32
F32R = mybir.dt.float32r
BF16 = mybir.dt.bfloat16
ALU = mybir.AluOpType
ACT = mybir.ActivationFunctionType
AX = mybir.AxisListType

B, S, D = 2, 2048, 256
H = 16
HD = D // H
HID = 1024
P = 128
TB = 512
NT = TB // P
BLOCKS = B * S // TB
QB = S // TB
ST = S // P
DC = D // P
HC = HID // P
GH = 4
HG = H // GH
GROUPS = B * HG
VW = 32
EPS = 1e-5
SCORE_SCALE = 1.0 / D ** 0.5

R_MIX = 3 * HD
R_CUT = R_MIX + 2 * QB
R_ALL = R_CUT + 2
HALF = 64
MASK = -1.0e30


STATS = 3


def layernorm_stats(nc, dve, x_of, st, mv, done, base):
    for t in range(NT):
        last = nc.vector.bn_stats(st[:, t, :], x_of(t))
    last.then_inc(done, 1)
    dve.wait_ge(done, base + 1)
    dve.sem_inc(done, 1)
    for t in range(NT):
        last = nc.vector.bn_aggr(mv[:, t, :], st[:, t, :])
    last.then_inc(done, 1)


def inverse_deviation(nc, pool, mv, tmp, rs, env, done, base):
    nc.gpsimd.tensor_tensor(tmp[:, :], mv[:, :, 1], env["eps"][:, :], ALU.add).then_inc(done, 1)
    pool.wait_ge(done, base + 1)
    nc.gpsimd.tensor_tensor(rs[:, :], tmp[:, :], env["neg_half"][:, :], ALU.pow).then_inc(done, 1)


def stage_projections(nc, env):
    consts, kqs, vs, mrows = env["consts"], env["kqs"], env["vs"], env["mrows"]
    x, w_kqv, m = env["x"], env["w_kqv"], env["m"]
    with ExitStack() as ctx:
        def sb(name, shape, dt=F32):
            return ctx.enter_context(nc.sbuf_tensor(f"qkv_{name}", shape, dt))

        def bank(name, shape=(P, TB)):
            return ctx.enter_context(nc.psum_tensor(f"qkv_{name}", list(shape), F32))

        def sem(name):
            return ctx.enter_context(nc.semaphore(f"qkv_{name}"))

        ident = consts[:, 0:P]
        sel = consts[:, 3 * P:3 * P + 8]
        w_raw = sb("w_raw", [P, DC, 3 * D])
        w_hi = sb("w_hi", [P, DC, 3 * D], F32R)
        w_lo = sb("w_lo", [P, DC, 3 * D], F32R)
        m_col = sb("m_col", [P, 1])
        m_hi = sb("m_hi", [P, 1], F32R)
        m_lo = sb("m_lo", [P, 1])
        m_a = sb("m_a", [P, QB])
        m_b = sb("m_b", [P, QB])
        m_wide = sb("m_wide", [P, QB, TB], F32R)
        xs = [sb(f"xs{u}", [P, NT, D]) for u in range(2)]
        xn = [sb(f"xn{u}", [P, NT, D]) for u in range(2)]
        st = [sb(f"st{u}", [P, NT, 6]) for u in range(2)]
        mv = [sb(f"mv{u}", [P, NT, 2]) for u in range(2)]
        tmp = [sb(f"tmp{u}", [P, NT]) for u in range(2)]
        rs = [sb(f"rs{u}", [P, NT]) for u in range(2)]
        xh = [sb(f"xh{u}", [P, DC, TB], F32R) for u in range(2)]
        xl = [sb(f"xl{u}", [P, DC, TB], F32R) for u in range(2)]
        kqh = [sb(f"kqh{u}", [P, 2 * DC, TB], F32R) for u in range(2)]
        kql = [sb(f"kql{u}", [P, 2 * DC, TB], F32R) for u in range(2)]
        vt = [sb(f"vt{u}", [P, NT, H, VW]) for u in range(2)]
        ps_x = [bank(f"ps_x{c}") for c in range(DC)]
        ps_kq = [bank(f"ps_kq{c}") for c in range(2 * DC)]
        ps_v = [bank(f"ps_v{c}", (P, 2, D)) for c in range(2)]

        w_in = sem("w_in")
        x_in = [sem(f"x_in{u}") for u in range(2)]
        w_hi_done = sem("w_hi_done")
        w_lo_done = sem("w_lo_done")
        m_done = sem("m_done")
        m_out = sem("m_out")
        stats = sem("stats")
        rstd = sem("rstd")
        xn_done = sem("xn_done")
        x_t = sem("x_t")
        xh_done = sem("xh_done")
        xl_done = sem("xl_done")
        kq_ps = sem("kq_ps")
        kqh_done = sem("kqh_done")
        kql_done = sem("kql_done")
        v_ps = sem("v_ps")
        v_done = sem("v_done")
        v_ones = sem("v_ones")
        stored = [sem(f"stored{u}") for u in range(2)]
        out_free = sem("out_free")
        half_done = sem("half_done")
        block = ctx.enter_context(nc.Block())
        x_blocks = x.rearrange("b (i t p) d -> (b i) p t d", p=P, t=NT)
        STORES = 2 * 2 * DC + NT

        @block.sync
        def _(sp):
            sp.dma_start(consts[:, :], env["consts_in"]).then_inc(w_in, 16)
            sp.dma_start(w_raw[:, :, :], w_kqv.rearrange("(c p) n -> p c n", p=P)).then_inc(w_in, 16)
            sp.dma_start(m_col[:, :], m.rearrange("h a b -> h (a b)").unsqueeze(1).broadcast_to([H, 8, 1])).then_inc(w_in, 16)
            sp.dma_start(env["ramp"][:, :], env["ramp_in"]).then_inc(w_in, 16)
            sp.sem_inc(out_free, 2)
            with sp.Fori(0, B) as b:
                with sp.Fori(0, QB // 2) as ii:
                    for u in range(2):
                        g = 4 * b + 2 * ii + u
                        sp.wait_ge(kql_done, 2 * DC * g + 4 * DC)
                        for c in range(2 * DC):
                            for part, src in enumerate((kqh, kql)):
                                dst = kqs[part, c // DC, bass.ds(b * D + (c % DC) * P, P), bass.ds(ii * 2 * TB + u * TB, TB)]
                                sp.dma_start(dst, src[u][:, c, :].bitcast(F32)).then_inc(stored[u], 16)
                        sp.wait_ge(v_done, 2 * g + 4)
                        for t in range(NT):
                            dst = vs[bass.ds(b * HG, HG), bass.ds(ii * 2 * TB + u * TB + t * P, P), :].rearrange("g p c -> p g c")
                            sp.dma_start(dst, vt[u][:, t, :, :].rearrange("p (g h) c -> p g (h c)", g=HG)).then_inc(stored[u], 16)
                        sp.wait_ge(stored[u], 16 * STORES * (2 * b + ii + 1))
                        sp.sem_inc(out_free, 1)
            sp.wait_ge(m_done, 5)
            for b in range(B):
                sp.dma_start(mrows[b * P:(b + 1) * P, :], m_wide[:, :, :].rearrange("p i q -> p (i q)").bitcast(F32)).then_inc(m_out, 16)
            sp.wait_ge(m_out, 16 * B)

        @block.gpsimd
        def _(pool):
            nc.gpsimd.memset(env["eps"][:, :], EPS)
            nc.gpsimd.memset(env["neg_half"][:, :], -0.5).then_inc(half_done, 1)
            for u in range(2):
                pool.dma_start(xs[u][:, :, :], x_blocks[u]).then_inc(x_in[u], 16)
            pool.wait_ge(half_done, 1)

            def one(g, u, load):
                pool.wait_ge(stats, STATS * g + STATS)
                inverse_deviation(nc, pool, mv[u], tmp[u], rs[u], env, rstd, 2 * g)
                if load:
                    pool.wait_ge(xn_done, g + 1)
                    pool.dma_start(xs[u][:, :, :], x_blocks[g + 2]).then_inc(x_in[u], 16)

            with pool.Fori(0, BLOCKS // 2 - 1) as r:
                for u in range(2):
                    one(2 * r + u, u, True)
            for u in range(2):
                one(BLOCKS - 2 + u, u, False)

        @block.vector
        def _(dve):
            for u in range(2):
                last = nc.vector.memset(vt[u][:, :, :, :], 0.0)
            last.then_inc(v_ones, 1)
            dve.wait_ge(v_ones, 1)
            for u in range(2):
                last = nc.vector.memset(vt[u][:, :, :, HD:HD + 1], 1.0)
            last.then_inc(v_ones, 1)
            dve.sem_inc(xl_done, DC)
            dve.sem_inc(kql_done, 2 * DC)
            dve.wait_ge(w_in, 64)
            dve.wait_ge(w_hi_done, 1)
            nc.vector.tensor_tensor(w_lo[:, :, :], w_raw[:, :, :], w_hi[:, :, :].bitcast(F32), ALU.subtract).then_inc(w_lo_done, 1)
            nc.vector.tensor_copy(env["ident_b"][:, :], ident)
            nc.vector.tensor_copy(env["mask_kq"][:, :], consts[:, P:2 * P])
            nc.vector.tensor_copy(env["mask_qk"][:, :], consts[:, 2 * P:3 * P])
            nc.vector.tensor_copy(env["ramp_r"][:, :], env["ramp"][:, :])
            nc.vector.tensor_copy(m_hi[:, :], m_col[:, :]).then_inc(m_done, 1)
            dve.wait_ge(m_done, 1)
            nc.vector.tensor_tensor(m_lo[:, :], m_col[:, :], m_hi[:, :].bitcast(F32), ALU.subtract).then_inc(m_done, 1)
            dve.wait_ge(m_done, 2)
            nc.vector.tensor_scalar(m_a[:, :], sel[:, 0:QB], m_hi[:, :].bitcast(F32), None, ALU.mult).then_inc(m_done, 1)
            dve.wait_ge(m_done, 3)
            nc.vector.scalar_tensor_tensor(m_b[:, :], sel[:, QB:2 * QB], m_lo[:, :], m_a[:, :], ALU.mult, ALU.add).then_inc(m_done, 1)
            dve.wait_ge(m_done, 4)
            nc.vector.tensor_copy(m_wide[:, :, :], m_b[:, :].unsqueeze(2).broadcast_to([P, QB, TB])).then_inc(m_done, 1)
            with dve.Fori(0, BLOCKS // 2) as r:
                for u in range(2):
                    g = 2 * r + u
                    dve.wait_ge(x_in[u], 16 * r + 16)
                    layernorm_stats(nc, dve, lambda t: xs[u][:, t, :], st[u], mv[u], stats, STATS * g)
                    dve.wait_ge(rstd, 2 * g + 2)
                    for t in range(NT):
                        last = nc.vector.tensor_scalar(xn[u][:, t, :], xs[u][:, t, :], mv[u][:, t, 0:1], rs[u][:, t:t + 1],
                                                       ALU.subtract, ALU.mult)
                    last.then_inc(xn_done, 1)
                    for c in range(DC):
                        dve.wait_ge(xh_done, DC * g + c + 1)
                        nc.vector.tensor_tensor(xl[u][:, c, :], ps_x[c][:, :], xh[u][:, c, :].bitcast(F32), ALU.subtract).then_inc(xl_done, 1)
                    dve.wait_ge(out_free, g + 1)
                    for c in range(2 * DC):
                        dve.wait_ge(kqh_done, 2 * DC * g + c + 1)
                        nc.vector.scalar_tensor_tensor(kql[u][:, c, :], ps_kq[c][:, :], 1.0 if c < DC else SCORE_SCALE,
                                                       kqh[u][:, c, :].bitcast(F32), ALU.mult, ALU.subtract).then_inc(kql_done, 1)

        @block.scalar
        def _(act):
            act.wait_ge(w_in, 64)
            nc.scalar.activation(w_hi[:, :, :], w_raw[:, :, :], ACT.Copy).then_inc(w_hi_done, 1)
            act.wait_ge(v_ones, 2)
            act.sem_inc(v_done, 2)
            with act.Fori(0, BLOCKS // 2) as r:
                for u in range(2):
                    g = 2 * r + u
                    for c in range(DC):
                        act.wait_ge(x_t, DC * g + c + 1)
                        nc.scalar.activation(xh[u][:, c, :], ps_x[c][:, :], ACT.Copy).then_inc(xh_done, 1)
                    act.wait_ge(out_free, g + 1)
                    for c in range(2 * DC):
                        act.wait_ge(kq_ps, 2 * DC * g + c + 1)
                        nc.scalar.activation(kqh[u][:, c, :], ps_kq[c][:, :], ACT.Copy,
                                             scale=1.0 if c < DC else SCORE_SCALE).then_inc(kqh_done, 1)
                    for v in range(2):
                        act.wait_ge(v_ps, 2 * g + v + 1)
                        nc.scalar.activation(vt[u][:, 2 * v:2 * v + 2, :, 0:HD],
                                             ps_v[v][:, :, :].rearrange("p t (h d) -> p t h d", d=HD), ACT.Copy).then_inc(v_done, 1)

        @block.tensor
        def _(pe):
            pe.wait_ge(w_lo_done, 1)
            with pe.Fori(0, BLOCKS // 2) as r:
                for u in range(2):
                    g = 2 * r + u
                    pe.wait_ge(xn_done, g + 1)
                    for c in range(DC):
                        pe.wait_ge(xl_done, DC * g + c + 1)
                        for t in range(NT):
                            last = nc.tensor.transpose(ps_x[c][:, t * P:(t + 1) * P], xn[u][:, t, c * P:(c + 1) * P], ident)
                        last.then_inc(x_t, 1)
                    pe.wait_ge(xl_done, DC * g + 2 * DC)
                    for c in range(2 * DC):
                        pe.wait_ge(kql_done, 2 * DC * g + c + 1)
                        n = 0
                        for k in range(DC):
                            for w, xx in ((w_hi, xh), (w_hi, xl), (w_lo, xh)):
                                last = nc.tensor.matmul(ps_kq[c][:, :], w[:, k, c * P:(c + 1) * P], xx[u][:, k, :],
                                                        start=(n == 0), stop=(n == 3 * DC - 1))
                                n += 1
                        last.then_inc(kq_ps, 1)
                    for v in range(2):
                        pe.wait_ge(v_done, 2 * g + v + 1)
                        for j in range(2):
                            n = 0
                            for k in range(DC):
                                for w, xx in ((w_hi, xh), (w_hi, xl), (w_lo, xh)):
                                    last = nc.tensor.matmul(ps_v[v][:, j, :], xx[u][:, k, (2 * v + j) * P:(2 * v + j + 1) * P],
                                                            w[:, k, 2 * D:3 * D], start=(n == 0), stop=(n == 3 * DC - 1))
                                    n += 1
                        last.then_inc(v_ps, 1)


RING = 3
MAX_UNITS = [(t, p, c, e) for t in range(ST) for p in range(GH // 2) for c in range(t // NT + 1) for e in range(2)]
STEPS = [(i, j) for i in range(QB) for j in range(NT * (i + 1))]
FIRST_MAX_STEP, LAST_MAX_STEP, CUT_STEP = 5, 36, 38
P_SLOTS = 4
UNITS_PROLOGUE = len(MAX_UNITS) + 1
UNITS_GROUP = UNITS_PROLOGUE + QB
LOADS = GH * 6 + GH + 2


def first_step(i):
    return NT * i * (i + 1) // 2


def group_schedule(with_max):
    out, units = [], list(MAX_UNITS) if with_max else []
    slots = LAST_MAX_STEP - FIRST_MAX_STEP + 1
    given = 0
    for s, (i, j) in enumerate(STEPS):
        out.append(("scores", s))
        if with_max and FIRST_MAX_STEP <= s <= LAST_MAX_STEP:
            upto = len(MAX_UNITS) * (s - FIRST_MAX_STEP + 1) // slots
            out += [("max", units[n]) for n in range(given, upto)]
            given = upto
        if with_max and s == CUT_STEP:
            out.append(("cut", None))
        if s:
            if s - 1 == first_step(STEPS[s - 1][0]) and s > 1:
                out.append(("turn", STEPS[s - 1][0] - 1))
            out.append(("values", s - 1))
    out += [("values", len(STEPS) - 1), ("turn", QB - 1)]
    return out


PROLOGUE = [("max", unit) for unit in MAX_UNITS] + [("cut", None)]


def stage_attention(nc, env):
    kqs, vs, mrows, att = env["kqs"], env["vs"], env["mrows"], env["att"]
    with ExitStack() as ctx:
        def sb(name, shape, dt=F32):
            return ctx.enter_context(nc.sbuf_tensor(f"att_{name}", shape, dt))

        def bank(name, shape=(P, TB)):
            return ctx.enter_context(nc.psum_tensor(f"att_{name}", list(shape), F32))

        def sem(name):
            return ctx.enter_context(nc.semaphore(f"att_{name}"))

        ident = env["consts"][:, 0:P]
        ks = [[sb(f"ks{u}{p}", [P, S], F32R) for p in range(2)] for u in range(2)]
        qs = [[sb(f"qs{u}{p}", [P, S], F32R) for p in range(2)] for u in range(2)]
        vg = [sb(f"vg{u}", [P, ST, GH * VW]) for u in range(2)]
        probs = [sb(f"probs{n}", [P, GH, TB]) for n in range(P_SLOTS)]
        part_max = sb("part_max", [P, GH, ST, QB])
        neg_max = sb("neg_max", [P, 2 * GH, ST])
        cut_hi = sb("cut_hi", [GH * ST, P], F32R)
        cut_lo = sb("cut_lo", [GH * ST, P], F32R)
        o_t = sb("o_t", [P, TB])
        inv = sb("inv", [P, NT * GH])
        ps_s = [bank(f"ps_s{p}", (P, 2, TB)) for p in range(2)]
        ring = [bank(f"ring{n}") for n in range(RING)]
        ps_o = bank("ps_o")

        ramp_set = sem("ramp_set")
        loaded = [sem(f"loaded{u}") for u in range(2)]
        cut_set = sem("cut_set")
        scores_ps = sem("scores_ps")
        exp_done = sem("exp_done")
        pv_done = sem("pv_done")
        o_copied = sem("o_copied")
        ring_ps = sem("ring_ps")
        ring_used = sem("ring_used")
        max_done = sem("max_done")
        cut_part = sem("cut_part")
        inv_done = sem("inv_done")
        block = ctx.enter_context(nc.Block())

        def loads(sp, n, u):
            for h in range(GH):
                p, base = h // 2, HALF * (h % 2)
                for which, stack, parts in ((0, ks, (0, 0, 1)), (1, qs, (0, 1, 0))):
                    for k, part in enumerate(parts):
                        sp.dma_start(stack[u][p][base + k * HD:base + (k + 1) * HD, :].bitcast(F32),
                                     kqs[part, which, bass.ds(n * GH * HD + h * HD, HD), :]).then_inc(loaded[u], 16)
                sp.dma_start(qs[u][p][base + R_MIX:base + R_CUT, :].bitcast(F32),
                             mrows[bass.ds(n * GH * 8 + h * 8, 8), :]).then_inc(loaded[u], 16)
            for half in range(2):
                sp.dma_start(vg[u][:, half * ST // 2:(half + 1) * ST // 2, :],
                             vs[n, half * S // 2:(half + 1) * S // 2, :].rearrange("(t p) c -> p t c", p=P)).then_inc(loaded[u], 16)

        def cuts(sp, u, q_cut):
            sp.wait_ge(ring_used, q_cut + RING)
            for h in range(GH):
                p, base = h // 2, HALF * (h % 2)
                for k, src in enumerate((cut_hi, cut_lo)):
                    row = base + R_CUT + k
                    sp.dma_start(qs[u][p][row:row + 1, :].bitcast(F32), src[h * ST:(h + 1) * ST, :].bitcast(F32)).then_inc(cut_set, 16)

        def q_of(n):
            return 1 + UNITS_PROLOGUE + UNITS_GROUP * n

        cut_at = [k for k, (what, _) in enumerate([x for x in group_schedule(True) if x[0] in ("max", "cut", "turn")]) if what == "cut"][0]

        @block.sync
        def _(sp):
            for u in range(2):
                for p in range(2):
                    for e in range(2):
                        row = HALF * e + R_MIX
                        sp.dma_start(ks[u][p][row:row + 2 * QB + 2, :].bitcast(F32), env["ramp_r"][:, :].bitcast(F32)).then_inc(ramp_set, 16)
            loads(sp, 0, 0)
            loads(sp, 1, 1)
            cuts(sp, 0, len(MAX_UNITS) + 1)

            def group(n, u):
                cuts(sp, 1 - u, q_of(n) + cut_at)
                sp.wait_ge(pv_done, len(STEPS) * n + len(STEPS) + P_SLOTS)
                loads(sp, n + 2, u)

            with sp.Fori(0, GROUPS // 2 - 1) as r:
                for u in range(2):
                    group(2 * r + u, u)
            cuts(sp, 1, q_of(GROUPS - 2) + cut_at)

        @block.scalar
        def _(act):
            act.sem_inc(exp_done, 2)
            act.sem_inc(o_copied, 1)

            def group(n):
                for s, (i, j) in enumerate(STEPS):
                    skip = max(0, (j - NT * i) * P)
                    for p in range(2):
                        act.wait_ge(scores_ps, 2 * len(STEPS) * n + 2 * s + p + 1)
                        if p == 0:
                            act.wait_ge(pv_done, len(STEPS) * n + s + 1)
                        nc.scalar.activation(probs[s % P_SLOTS][:, 2 * p:2 * p + 2, skip:TB], ps_s[p][:, :, skip:TB],
                                             ACT.Exp).then_inc(exp_done, 1)
                    if s == first_step(i) and i > 0:
                        copy_out(n, i - 1)
                copy_out(n, QB - 1)

            def copy_out(n, i):
                last_step = first_step(i + 1) - 1
                act.wait_ge(pv_done, len(STEPS) * n + last_step + 1 + P_SLOTS)
                nc.scalar.activation(o_t[:, :], ps_o[:, :], ACT.Copy).then_inc(o_copied, 1)

            with act.Fori(0, GROUPS // 2 - 1) as r:
                for u in range(2):
                    group(2 * r + u)
            for n in range(GROUPS - 2, GROUPS):
                group(n)

        @block.vector
        def _(dve):
            nc.vector.memset(neg_max[:, GH:2 * GH, :], 0.0)
            dve.sem_inc(ring_used, RING)

            def unit(q, bank, what, arg, n, turned):
                dve.wait_ge(ring_ps, q)
                if what == "max":
                    t, p, c, e = arg
                    w = P * (t % NT + 1) if c == t // NT else TB
                    nc.vector.reduce_max(part_max[:, 2 * p + e, t, c:c + 1], ring[bank][:, 0:w], axis=AX.X).then_inc(ring_used, 1)
                elif what == "cut":
                    nc.vector.tensor_copy(cut_hi[:, :], ring[bank][0:GH * ST, 0:P]).then_inc(cut_part, 1)
                    dve.wait_ge(cut_part, n + 1)
                    nc.vector.tensor_tensor(cut_lo[:, :], ring[bank][0:GH * ST, 0:P], cut_hi[:, :].bitcast(F32),
                                            ALU.subtract).then_inc(ring_used, 1)
                else:
                    o = ring[bank][:, :].rearrange("p (g c) -> p g c", c=VW)
                    dve.wait_ge(ring_used, q - 1 + RING)
                    nc.vector.reciprocal(inv[:, :], o[:, :, HD]).then_inc(inv_done, 1)
                    dve.wait_ge(inv_done, QB * n + turned + 1)
                    dst = att[:, bass.ds(n // HG * ST + NT * arg, NT), bass.ds(n % HG * (GH * HD), GH * HD)].rearrange("p t (h d) -> p t h d", d=HD)
                    nc.vector.tensor_tensor(dst, o[:, :, 0:HD].rearrange("p (t h) d -> p t h d", h=GH),
                                            inv[:, :].rearrange("p (t h) -> p t h", h=GH).unsqueeze(3).broadcast_to([P, NT, GH, HD]),
                                            ALU.mult).then_inc(ring_used, 1)

            def finish_max(q):
                dve.wait_ge(ring_used, q - 1 + RING)
                for i in range(QB):
                    last = nc.vector.tensor_reduce(neg_max[:, 0:GH, NT * i:NT * (i + 1)], part_max[:, :, NT * i:NT * (i + 1), 0:i + 1],
                                                   op=ALU.max, axis=AX.X, negate=True)
                last.then_inc(max_done, 1)

            def run(schedule, q0, bank0, n, cut_n):
                k = turned = 0
                for what, arg in schedule:
                    if what in ("scores", "values"):
                        continue
                    if what == "cut":
                        finish_max(q0 + k)
                    q, bank = q0 + k, (bank0 + k) % RING
                    unit(q, bank, what, arg, cut_n if what == "cut" else n, turned)
                    turned += what == "turn"
                    k += 1

            run(PROLOGUE, 1, 1, 0, 0)
            with dve.Fori(0, GROUPS // 2 - 1) as r:
                for u in range(2):
                    n = 2 * r + u
                    run(group_schedule(True), q_of(n), 0, n, n + 1)
            run(group_schedule(True), q_of(GROUPS - 2), 0, GROUPS - 2, GROUPS - 1)
            run(group_schedule(False), q_of(GROUPS - 1), 0, GROUPS - 1, None)

        @block.tensor
        def _(pe):
            pe.sem_inc(pv_done, P_SLOTS)
            pe.wait_ge(ramp_set, 16 * 8)

            def scores(n, u, s):
                i, j = STEPS[s]
                skip = max(0, (j - NT * i) * P)
                for p in range(2):
                    pe.wait_ge(exp_done, 2 * len(STEPS) * n + 2 * s + p + 1)
                    for e in range(2):
                        rows = slice(HALF * e, HALF * e + R_ALL)
                        last = nc.tensor.matmul(ps_s[p][:, e, skip:TB], ks[u][p][rows, j * P:(j + 1) * P],
                                                qs[u][p][rows, i * TB + skip:(i + 1) * TB], start=True, stop=j < NT * i)
                    if j >= NT * i:
                        for e in range(2):
                            last = nc.tensor.matmul(ps_s[p][:, e, skip:skip + P], env["ident_b"][:, :], env["mask_kq"][:, :],
                                                    start=False, stop=True)
                    last.then_inc(scores_ps, 1)

            def values(n, u, s):
                i, j = STEPS[s]
                skip = max(0, (j - NT * i) * P)
                pe.wait_ge(exp_done, 2 * len(STEPS) * n + 2 * s + 2 + 2)
                if j == 0:
                    pe.wait_ge(o_copied, QB * n + i + 1)
                for h in range(GH):
                    last = nc.tensor.matmul(ps_o[VW * h:VW * (h + 1), skip:TB], vg[u][:, j, VW * h:VW * (h + 1)],
                                            probs[s % P_SLOTS][:, h, skip:TB], start=(j == 0), stop=(j == NT * (i + 1) - 1))
                last.then_inc(pv_done, 1)

            def unit(q, bank, what, arg, n, u):
                pe.wait_ge(ring_used, q)
                if what == "max":
                    t, p, c, e = arg
                    w = P * (t % NT + 1) if c == t // NT else TB
                    rows = slice(HALF * e, HALF * e + R_CUT)
                    diagonal = c == t // NT
                    last = nc.tensor.matmul(ring[bank][:, 0:w], qs[u][p][rows, t * P:(t + 1) * P],
                                            ks[u][p][rows, c * TB:c * TB + w], start=True, stop=not diagonal)
                    if diagonal:
                        last = nc.tensor.matmul(ring[bank][:, w - P:w], env["ident_b"][:, :], env["mask_qk"][:, :],
                                                start=False, stop=True)
                elif what == "cut":
                    pe.wait_ge(max_done, n + 1)
                    last = nc.tensor.transpose(ring[bank][:, 0:P], neg_max[:, :, :].rearrange("p h t -> p (h t)"), ident)
                else:
                    pe.wait_ge(o_copied, QB * n + arg + 2)
                    for t in range(NT):
                        last = nc.tensor.transpose(ring[bank][:, t * P:(t + 1) * P], o_t[:, t * P:(t + 1) * P], ident)
                last.then_inc(ring_ps, 1)

            def group(n, u, with_max):
                k = 0
                pe.wait_ge(cut_set, 16 * 2 * GH * n + 16 * 2 * GH)
                for what, arg in group_schedule(with_max):
                    if what == "scores":
                        scores(n, u, arg)
                    elif what == "values":
                        values(n, u, arg)
                    else:
                        if what == "max" and arg == MAX_UNITS[0]:
                            pe.wait_ge(loaded[1 - u], load_count(n + 1, u))
                        unit(q_of(n) + k, k % RING, what, arg, n if what == "turn" else n + 1, u if what == "turn" else 1 - u)
                        k += 1

            def load_count(n1, u):
                return 8 * LOADS * n1 + (8 * LOADS if u == 0 else 16 * LOADS)

            pe.wait_ge(loaded[0], 16 * LOADS)
            for k, (what, arg) in enumerate(PROLOGUE):
                unit(1 + k, (1 + k) % RING, what, arg, 0, 0)
            with pe.Fori(0, GROUPS // 2 - 1) as r:
                for u in range(2):
                    group(2 * r + u, u, True)
            group(GROUPS - 2, 0, True)
            group(GROUPS - 1, 1, False)


W_PIECE = HID


def load_weights(nc, pieces, stage, w_in, w_hi_done, w_lo_done):
    def sync(sp):
        for n, (src, _, _) in enumerate(pieces):
            if n >= 2:
                sp.wait_ge(w_lo_done, n - 1)
            sp.dma_start(stage[n % 2], src).then_inc(w_in[n % 2], 16)

    def scalar(act):
        for n, (_, hi, _) in enumerate(pieces):
            act.wait_ge(w_in[n % 2], 16 * (n // 2 + 1))
            nc.scalar.activation(hi, stage[n % 2], ACT.Copy).then_inc(w_hi_done, 1)

    def vector(dve):
        for n, (_, hi, lo) in enumerate(pieces):
            dve.wait_ge(w_hi_done, n + 1)
            nc.vector.tensor_tensor(lo, stage[n % 2], hi.bitcast(F32), ALU.subtract).then_inc(w_lo_done, 1)

    return sync, scalar, vector


def dense_512(nc, out, w_hi, w_lo, x_hi, x_lo, chunks, o):
    n = 0
    for c in range(chunks):
        for w, xx in ((w_hi, x_hi), (w_hi, x_lo), (w_lo, x_hi)):
            last = nc.tensor.matmul(out, w[:, c, o * P:(o + 1) * P], xx[:, c, :], start=(n == 0), stop=(n == 3 * chunks - 1))
            n += 1
    return last


def stage_ffn_in(nc, env):
    x, att, x1, h2 = env["x"], env["att"], env["x1"], env["h2"]
    with ExitStack() as ctx:
        def sb(name, shape, dt=F32):
            return ctx.enter_context(nc.sbuf_tensor(f"fin_{name}", shape, dt))

        def bank(name, shape=(P, TB)):
            return ctx.enter_context(nc.psum_tensor(f"fin_{name}", list(shape), F32))

        def sem(name):
            return ctx.enter_context(nc.semaphore(f"fin_{name}"))

        ident = env["consts"][:, 0:P]
        w1h, w1l, w2h, w2l = (sb(n, [P, DC, HID], F32R) for n in ("w1h", "w1l", "w2h", "w2l"))
        h1h, h1l = (sb(n, [P, HC, HID], F32R) for n in ("h1h", "h1l"))
        scales = sb("scales", [P, 4, HC])
        xs = sb("xs", [P, NT, D])
        xo = sb("xo", [P, NT, D])
        xn = sb("xn", [P, NT, D])
        st, mv, tmp, rs = sb("st", [P, NT, 6]), sb("mv", [P, NT, 2]), sb("tmp", [P, NT]), sb("rs", [P, NT])
        xh, xl = sb("xh", [P, DC, TB], F32R), sb("xl", [P, DC, TB], F32R)
        gate = [sb(f"gate{n}", [P, TB]) for n in range(2)]
        hf = [sb(f"hf{n}", [P, TB]) for n in range(2)]
        hh, hl = sb("hh", [P, HC, TB], F32R), sb("hl", [P, HC, TB], F32R)
        HALFC = HC // 2
        ho = sb("ho", [P, HALFC, TB])
        ps_x = [bank(f"ps_x{c}") for c in range(DC)]
        ps_1 = [bank(f"ps_1{n}", (P, 2, TB)) for n in range(2)]
        ps_2 = [bank(f"ps_2{n}") for n in range(2)]

        w_in = [sem(f"w_in{n}") for n in range(2)]
        names = ("w_hi_done w_lo_done s_in x_in stats rstd a_done x1_done xn_done x1_out x_t xh_done xl_done l1_ps gate_done "
                 "hf_done hh_done hl_done l2_ps gelu_done h2_out h2_free")
        (w_hi_done, w_lo_done, s_in, x_in, stats, rstd, a_done, x1_done, xn_done, x1_out, x_t, xh_done, xl_done, l1_ps, gate_done,
         hf_done, hh_done, hl_done, l2_ps, gelu_done, h2_out, h2_free) = (sem(n) for n in names.split())
        pieces = []
        for src, hi, lo, chunks in ((env["w1"], w1h, w1l, DC), (env["w2"], w2h, w2l, DC), (env["h1"], h1h, h1l, HC)):
            pieces += [(src[c * P:(c + 1) * P, :], hi[:, c, :], lo[:, c, :]) for c in range(chunks)]
        stage = [ho[:, 2 * n:2 * n + 2, :].rearrange("p a b -> p (a b)") for n in range(2)]
        w_sync, w_scalar, w_vector = load_weights(nc, pieces, stage, w_in, w_hi_done, w_lo_done)
        block = ctx.enter_context(nc.Block())
        x_blocks = x.rearrange("b (i t p) d -> (b i) p t d", p=P, t=NT)
        LAST = BLOCKS - 1

        @block.sync
        def _(sp):
            sp.dma_start(scales[:, :, :], env["scales"]).then_inc(s_in, 16)
            sp.dma_start(xs[:, :, :], x_blocks[0]).then_inc(x_in, 16)
            w_sync(sp)
            sp.sem_inc(h2_free, 1)
            sp.wait_ge(x1_done, 1)
            sp.dma_start(x1[0], xo[:, :, :]).then_inc(x1_out, 16)
            sp.dma_start(xs[:, :, :], x_blocks[1]).then_inc(x_in, 16)

            def body(g, last):
                if not last:
                    sp.wait_ge(x1_done, g + 2)
                    sp.dma_start(x1[g + 1], xo[:, :, :]).then_inc(x1_out, 16)
                for k in range(2):
                    sp.wait_ge(gelu_done, HC * g + HALFC * (k + 1) + 2)
                    sp.dma_start(h2[g, :, HALFC * k:HALFC * (k + 1), :], ho[:, :, :]).then_inc(h2_out, 16)
                    sp.wait_ge(h2_out, 32 * g + 16 * (k + 1))
                    sp.sem_inc(h2_free, 1)

            with sp.Fori(0, LAST - 1) as g:
                sp.wait_ge(x1_done, g + 2)
                sp.dma_start(xs[:, :, :], x_blocks[g + 2]).then_inc(x_in, 16)
                body(g, False)
            body(LAST - 1, False)
            body(LAST, True)
            sp.wait_ge(x1_out, 16 * BLOCKS)

        @block.gpsimd
        def _(pool):
            with pool.Fori(0, 2 * BLOCKS) as k:
                pool.wait_ge(stats, STATS * k + STATS)
                inverse_deviation(nc, pool, mv, tmp, rs, env, rstd, 2 * k)

        @block.scalar
        def _(act):
            w_scalar(act)
            act.wait_ge(s_in, 16)
            act.sem_inc(gelu_done, 2)

            def x_parts(g):
                for c in range(DC):
                    act.wait_ge(x_t, DC * g + c + 1)
                    nc.scalar.activation(xh[:, c, :], ps_x[c][:, :], ACT.Copy).then_inc(xh_done, 1)

            def body(g, last):
                for o in range(HC):
                    act.wait_ge(l1_ps, HC * g + o + 1)
                    nc.scalar.activation(gate[o % 2][:, :], ps_1[o % 2][:, 0, :], ACT.Silu, scale=scales[:, 0, o:o + 1]).then_inc(gate_done, 1)
                    act.wait_ge(hf_done, HC * g + o + 1)
                    nc.scalar.activation(hh[:, o, :], hf[o % 2][:, :], ACT.Copy).then_inc(hh_done, 1)
                for o in range(HC):
                    if o % HALFC == 0:
                        act.wait_ge(h2_free, 2 * g + o // HALFC + 1)
                    act.wait_ge(l2_ps, HC * g + o + 1)
                    nc.scalar.activation(ho[:, o % HALFC, :], ps_2[o % 2][:, :], ACT.Gelu, scale=scales[:, 2, o:o + 1]).then_inc(gelu_done, 1)
                    if o == HALFC - 1 and not last:
                        x_parts(g + 1)

            x_parts(0)
            with act.Fori(0, LAST) as g:
                body(g, False)
            body(LAST, True)

        @block.vector
        def _(dve):
            dve.sem_inc(hl_done, 2)

            def prepare(g, first=False):
                a = att[:, bass.ds(g * NT, NT), :]
                dve.wait_ge(x_in, 16 * g + 16)
                layernorm_stats(nc, dve, lambda t: a[:, t, :], st, mv, stats, 2 * STATS * g)
                dve.wait_ge(rstd, 4 * g + 2)
                for t in range(NT):
                    last = nc.vector.tensor_scalar(xn[:, t, :], a[:, t, :],
                                                   mv[:, t, 0:1], rs[:, t:t + 1], ALU.subtract, ALU.mult)
                last.then_inc(a_done, 1)
                dve.wait_ge(a_done, g + 1)
                if not first:
                    dve.wait_ge(x1_out, 16 * g)
                nc.vector.tensor_tensor(xo[:, :, :], xn[:, :, :], xs[:, :, :], ALU.add).then_inc(x1_done, 1)
                dve.wait_ge(x1_done, g + 1)
                layernorm_stats(nc, dve, lambda t: xo[:, t, :], st, mv, stats, 2 * STATS * g + STATS)
                dve.wait_ge(rstd, 4 * g + 4)
                for t in range(NT):
                    last = nc.vector.tensor_scalar(xn[:, t, :], xo[:, t, :], mv[:, t, 0:1], rs[:, t:t + 1], ALU.subtract, ALU.mult)
                last.then_inc(xn_done, 1)

            def x_parts(g):
                for c in range(DC):
                    dve.wait_ge(xh_done, DC * g + c + 1)
                    nc.vector.tensor_tensor(xl[:, c, :], ps_x[c][:, :], xh[:, c, :].bitcast(F32), ALU.subtract).then_inc(xl_done, 1)

            def layer1(g):
                for o in range(HC):
                    dve.wait_ge(gate_done, HC * g + o + 1)
                    nc.vector.scalar_tensor_tensor(hf[o % 2][:, :], ps_1[o % 2][:, 1, :], scales[:, 1, o:o + 1], gate[o % 2][:, :],
                                                   ALU.mult, ALU.mult).then_inc(hf_done, 1)
                    dve.wait_ge(hh_done, HC * g + o + 1)
                    nc.vector.tensor_tensor(hl[:, o, :], hf[o % 2][:, :], hh[:, o, :].bitcast(F32), ALU.subtract).then_inc(hl_done, 1)

            prepare(0, first=True)
            w_vector(dve)
            x_parts(0)
            with dve.Fori(0, LAST) as g:
                layer1(g)
                prepare(g + 1)
                x_parts(g + 1)
            layer1(LAST)

        @block.tensor
        def _(pe):
            def turn(g):
                pe.wait_ge(xn_done, g + 1)
                for c in range(DC):
                    for t in range(NT):
                        last = nc.tensor.transpose(ps_x[c][:, t * P:(t + 1) * P], xn[:, t, c * P:(c + 1) * P], ident)
                    last.then_inc(x_t, 1)

            def body(g, last_block):
                pe.wait_ge(xh_done, DC * g + DC)
                pe.wait_ge(xl_done, DC * g + DC)
                for o in range(HC):
                    pe.wait_ge(hl_done, HC * g + o + 1)
                    dense_512(nc, ps_1[o % 2][:, 0, :], w1h, w1l, xh, xl, DC, o)
                    dense_512(nc, ps_1[o % 2][:, 1, :], w2h, w2l, xh, xl, DC, o).then_inc(l1_ps, 1)
                pe.wait_ge(hl_done, HC * g + HC + 2)
                for o in range(HC):
                    pe.wait_ge(gelu_done, HC * g + o + 1)
                    dense_512(nc, ps_2[o % 2][:, :], h1h, h1l, hh, hl, HC, o).then_inc(l2_ps, 1)
                    if o == HALFC - 1 and not last_block:
                        turn(g + 1)

            turn(0)
            pe.wait_ge(w_lo_done, len(pieces))
            with pe.Fori(0, LAST) as g:
                body(g, False)
            body(LAST, True)


def stage_ffn_out(nc, env):
    x1, h2, out = env["x1"], env["h2"], env["out"]
    with ExitStack() as ctx:
        def sb(name, shape, dt=F32):
            return ctx.enter_context(nc.sbuf_tensor(f"fout_{name}", shape, dt))

        def bank(name, shape=(P, TB)):
            return ctx.enter_context(nc.psum_tensor(f"fout_{name}", list(shape), F32))

        def sem(name):
            return ctx.enter_context(nc.semaphore(f"fout_{name}"))

        h2h, h2l = (sb(n, [P, HC, HID], F32R) for n in ("h2h", "h2l"))
        w3h, w3l = (sb(n, [P, HC, D], F32R) for n in ("w3h", "w3l"))
        scales = sb("scales2", [P, HC])
        s3 = sb("s3", [P, D])
        hin = sb("hin", [P, HC, TB])
        ah, al = sb("ah", [P, HC, TB], F32R), sb("al", [P, HC, TB], F32R)
        hf = [sb(f"hg{n}", [P, TB]) for n in range(2)]
        bh, bl = sb("bh", [P, HC, TB], F32R), sb("bl", [P, HC, TB], F32R)
        xr = sb("xr", [P, NT, D])
        y = sb("y", [P, NT, D])
        yo = sb("yo", [P, NT, D])
        st, mv, tmp, rs = sb("st", [P, NT, 6]), sb("mv", [P, NT, 2]), sb("tmp", [P, NT]), sb("rs", [P, NT])
        ps_3 = [bank(f"ps_3{n}") for n in range(4)]
        ps_y = [bank(f"ps_y{n}") for n in range(4)]
        w_in = [sem(f"v_in{n}") for n in range(2)]
        names = ("w_hi_done2 w_lo_done2 s_in2 h_in x_in2 stats2 rstd2 ah_done al_done l3_ps gelu_done2 bh_done bl_done "
                 "y_ps y_done n_done o_done out_done")
        (w_hi_done, w_lo_done, s_in, h_in, x_in, stats, rstd, ah_done, al_done, l3_ps, gelu_done, bh_done, bl_done,
         y_ps, y_done, n_done, o_done, out_done) = (sem(n) for n in names.split())
        pieces = [(env["h2w"][c * P:(c + 1) * P, :], h2h[:, c, :], h2l[:, c, :]) for c in range(HC)]
        pieces += [(env["w3"][c * NT * P:(c + 1) * NT * P, :].rearrange("(t p) n -> p t n", p=P), w3h[:, c * NT:(c + 1) * NT, :],
                    w3l[:, c * NT:(c + 1) * NT, :]) for c in range(HC // NT)]
        flat = [bh_raw[:, :] for bh_raw in (sb("stage0", [P, W_PIECE]), sb("stage1", [P, W_PIECE]))]
        block = ctx.enter_context(nc.Block())
        LAST = BLOCKS - 1
        out_blocks = out.rearrange("b (i t p) d -> (b i) p t d", p=P, t=NT)

        def staged(n):
            v = flat[n % 2]
            return v if n < HC else v.rearrange("p (t n) -> p t n", t=NT)

        @block.sync
        def _(sp):
            sp.dma_start(scales[:, :], env["scales"][:, 3, :]).then_inc(s_in, 16)
            sp.dma_start(s3[:, :], env["s3"].partition_broadcast(P)).then_inc(s_in, 16)
            sp.dma_start(hin[:, :, :], h2[0]).then_inc(h_in, 16)
            for n, (src, _, _) in enumerate(pieces):
                if n >= 2:
                    sp.wait_ge(w_lo_done, n - 1)
                sp.dma_start(staged(n), src).then_inc(w_in[n % 2], 16)
            sp.dma_start(xr[:, :, :], x1[0]).then_inc(x_in, 16)

            def body(g, last):
                if not last:
                    sp.wait_ge(al_done, HC // 2 * g + HC // 2)
                    sp.dma_start(hin[:, :, :], h2[g + 1]).then_inc(h_in, 16)
                sp.wait_ge(o_done, g + 1)
                sp.dma_start(out_blocks[g], yo[:, :, :]).then_inc(out_done, 16)
                if not last:
                    sp.dma_start(xr[:, :, :], x1[g + 1]).then_inc(x_in, 16)

            with sp.Fori(0, LAST) as g:
                body(g, False)
            body(LAST, True)
            sp.wait_ge(out_done, 16 * BLOCKS)

        @block.gpsimd
        def _(pool):
            with pool.Fori(0, BLOCKS) as k:
                pool.wait_ge(stats, STATS * k + STATS)
                inverse_deviation(nc, pool, mv, tmp, rs, env, rstd, 2 * k)

        @block.scalar
        def _(act):
            for n, (_, hi, _) in enumerate(pieces):
                act.wait_ge(w_in[n % 2], 16 * (n // 2 + 1))
                nc.scalar.activation(hi, staged(n), ACT.Copy).then_inc(w_hi_done, 1)
            act.wait_ge(s_in, 32)
            act.sem_inc(gelu_done, 4)

            def split(g):
                act.wait_ge(h_in, 16 * g + 16)
                for c in range(0, HC, 2):
                    nc.scalar.activation(ah[:, c:c + 2, :], hin[:, c:c + 2, :], ACT.Copy).then_inc(ah_done, 1)

            def body(g, last):
                for o in range(HC):
                    act.wait_ge(l3_ps, HC * g + o + 1)
                    act.wait_ge(bl_done, HC * g + o + 1)
                    nc.scalar.activation(hf[o % 2][:, :], ps_3[o % 4][:, :], ACT.Gelu, scale=scales[:, o:o + 1]).then_inc(gelu_done, 1)
                    act.wait_ge(gelu_done, HC * g + o + 5)
                    nc.scalar.activation(bh[:, o, :], hf[o % 2][:, :], ACT.Copy).then_inc(bh_done, 1)
                if not last:
                    split(g + 1)

            split(0)
            with act.Fori(0, LAST) as g:
                body(g, False)
            body(LAST, True)

        @block.vector
        def _(dve):
            for n, (_, hi, lo) in enumerate(pieces):
                dve.wait_ge(w_hi_done, n + 1)
                nc.vector.tensor_tensor(lo, staged(n), hi.bitcast(F32), ALU.subtract).then_inc(w_lo_done, 1)
            dve.sem_inc(bl_done, 2)
            dve.sem_inc(y_done, NT)
            dve.wait_ge(s_in, 32)

            def split(g):
                for c in range(0, HC, 2):
                    dve.wait_ge(ah_done, HC // 2 * g + c // 2 + 1)
                    nc.vector.tensor_tensor(al[:, c:c + 2, :], hin[:, c:c + 2, :], ah[:, c:c + 2, :].bitcast(F32), ALU.subtract).then_inc(al_done, 1)

            def body(g, last_block, first=False):
                for o in range(HC):
                    dve.wait_ge(bh_done, HC * g + o + 1)
                    nc.vector.tensor_tensor(bl[:, o, :], hf[o % 2][:, :], bh[:, o, :].bitcast(F32), ALU.subtract).then_inc(bl_done, 1)
                if not last_block:
                    split(g + 1)
                for t in range(NT):
                    dve.wait_ge(y_ps, NT * g + t + 1)
                    nc.vector.tensor_tensor(y[:, t, :], ps_y[t][:, 0:D], s3[:, :], ALU.mult).then_inc(y_done, 1)
                dve.wait_ge(y_done, NT * g + 2 * NT)
                layernorm_stats(nc, dve, lambda t: y[:, t, :], st, mv, stats, STATS * g)
                dve.wait_ge(rstd, 2 * g + 2)
                if not first:
                    dve.wait_ge(out_done, 16 * g)
                for t in range(NT):
                    last = nc.vector.tensor_scalar(yo[:, t, :], y[:, t, :], mv[:, t, 0:1], rs[:, t:t + 1], ALU.subtract, ALU.mult)
                last.then_inc(n_done, 1)
                dve.wait_ge(n_done, g + 1)
                dve.wait_ge(x_in, 16 * g + 16)
                nc.vector.tensor_tensor(yo[:, :, :], yo[:, :, :], xr[:, :, :], ALU.add).then_inc(o_done, 1)

            split(0)
            body(0, False, first=True)
            with dve.Fori(1, LAST) as g:
                body(g, False)
            body(LAST, True)

        @block.tensor
        def _(pe):
            def body(g):
                pe.wait_ge(al_done, HC // 2 * g + HC // 2)
                for o in range(HC):
                    pe.wait_ge(gelu_done, HC * g + o + 1)
                    dense_512(nc, ps_3[o % 4][:, :], h2h, h2l, ah, al, HC, o).then_inc(l3_ps, 1)
                for t in range(NT):
                    pe.wait_ge(y_done, NT * g + t + 1)
                    n = 0
                    for c in range(HC):
                        if t == 0:
                            pe.wait_ge(bl_done, HC * g + c + 3)
                        for a, w in ((bh, w3h), (bl, w3h), (bh, w3l)):
                            last = nc.tensor.matmul(ps_y[t][:, 0:D], a[:, c, t * P:(t + 1) * P], w[:, c, :],
                                                    start=(n == 0), stop=(n == 3 * HC - 1))
                            n += 1
                    last.then_inc(y_ps, 1)

            pe.wait_ge(w_lo_done, len(pieces))
            with pe.Fori(0, BLOCKS) as g:
                body(g)


def build(nc, x, w_kqv, m, w1, w2, h1, h2w, w3, scales, s3, consts_in, ramp_in, out):
    env = dict(x=x, w_kqv=w_kqv, m=m, w1=w1, w2=w2, h1=h1, h2w=h2w, w3=w3, scales=scales, s3=s3, out=out,
               consts_in=consts_in, ramp_in=ramp_in)
    env["kqs"] = nc.dram_tensor("kqs", [2, 2, B * D, S], F32).ap()
    env["vs"] = nc.dram_tensor("vs", [GROUPS, S, GH * VW], F32).ap()
    env["mrows"] = nc.dram_tensor("mrows", [B * P, S], F32).ap()
    env["x1"] = nc.dram_tensor("x1", [BLOCKS, P, NT, D], F32).ap()
    env["h2"] = nc.dram_tensor("h2", [BLOCKS, P, HC, TB], F32).ap()
    with (
        nc.sbuf_tensor("consts", [P, 3 * P + 8], F32) as consts,
        nc.sbuf_tensor("ident_b", [P, P], BF16) as ident_b,
        nc.sbuf_tensor("mask_kq", [P, P], BF16) as mask_kq,
        nc.sbuf_tensor("mask_qk", [P, P], BF16) as mask_qk,
        nc.sbuf_tensor("neg_half", [P, NT], F32) as neg_half,
        nc.sbuf_tensor("eps", [P, NT], F32) as eps,
    ):
        env.update(consts=consts, ident_b=ident_b, mask_kq=mask_kq, mask_qk=mask_qk, neg_half=neg_half, eps=eps)
        with nc.sbuf_tensor("att", [P, BLOCKS * NT, D], F32) as att:
            env["att"] = att
            with nc.sbuf_tensor("ramp", [2 * QB + 2, S], F32) as ramp, nc.sbuf_tensor("ramp_r", [2 * QB + 2, S], F32R) as ramp_r:
                env.update(ramp=ramp, ramp_r=ramp_r)
                stage_projections(nc, env)
                stage_attention(nc, env)
            stage_ffn_in(nc, env)
        stage_ffn_out(nc, env)


def kernel(**inputs):
    import numpy as np
    import concourse.bacc as bacc
    from concourse import mybir as _mybir
    from concourse.bass_utils import run_bass_kernel_spmd

    get = {k.removeprefix("L0_"): np.asarray(v) for k, v in inputs.items()}
    consts = np.zeros((P, 3 * P + 8), np.float32)
    consts[:, 0:P] = np.eye(P)
    consts[:, P:2 * P] = np.tril(np.full((P, P), MASK), -1)
    consts[:, 2 * P:3 * P] = np.triu(np.full((P, P), MASK), 1)
    consts[:, 3 * P:] = np.tile(np.eye(8), (P // 8, 1))
    ramp = np.ones((2 * QB + 2, S), np.float32)
    for i in range(QB):
        ramp[i] = ramp[QB + i] = np.arange(S) - (TB * i + TB // 2)
    turned = {k: np.ascontiguousarray(get[f"ffn_{k}_w"].T) for k in ("w1", "w2", "h1", "h2", "w3")}
    scales = np.stack([get[f"ffn_{k}_s"].reshape(HC, P).T for k in ("w1", "w2", "h1", "h2")], 1)
    arrays = dict(x=get["attn_x"], w_kqv=get["attn_W_kqv"], m=get["attn_m"], w1=turned["w1"], w2=turned["w2"], h1=turned["h1"],
                  h2w=turned["h2"], w3=turned["w3"], scales=scales, s3=get["ffn_w3_s"], consts_in=consts, ramp_in=ramp)
    arrays = {f"in_{k}": np.ascontiguousarray(v) for k, v in arrays.items()}
    nc = bacc.Bacc("TRN2", target_bir_lowering=False, num_devices=1)
    args = [nc.dram_tensor(k, v.shape, _mybir.dt.from_np(v.dtype), kind="ExternalInput").ap() for k, v in arrays.items()]
    args.append(nc.dram_tensor("out_0", (B, S, D), F32, kind="ExternalOutput").ap())
    build(nc, *args)
    return run_bass_kernel_spmd(nc, [arrays], core_ids=[0]).results[0]["out_0"]
```

```python
import concourse.bass as bass
from concourse import mybir
from contextlib import ExitStack

F32 = mybir.dt.float32
F32R = mybir.dt.float32r
BF16 = mybir.dt.bfloat16
ALU = mybir.AluOpType
ACT = mybir.ActivationFunctionType
AX = mybir.AxisListType
RMAX = bass.bass_isa.ReduceOp.max

B, S, D = 2, 2048, 256
H = 16
HD = D // H
HID = 1024
P = 128
TB = 512
NT = TB // P
BLOCKS = B * S // TB
QB = S // TB
ST = S // P
DC = D // P
HC = HID // P
GH = 4
HG = H // GH
GROUPS = B * HG
VW = 32
EPS = 1e-5
SCORE_SCALE = 1.0 / D ** 0.5

R_MIX = 3 * HD
R_CUT = R_MIX + 2 * QB
R_ALL = R_CUT + 2
HALF = 64
MASK = -1.0e30


LOADS = 4 * GH + 2
RAMPS = GH


def load_ramp(eng, env, u):
    for h in range(GH):
        row = HALF * (h % 2) + R_MIX
        eng.dma_start(env["ks"][u][h // 2][row:row + 2 * QB + 2, :].bitcast(F32), env["ramp_r"][:, :].bitcast(F32)).then_inc(env["ramp_set"][u], 16)


def load_group(eng, env, n, u):
    kst, qst, vs, loaded = env["kst"], env["qst"], env["vs"], env["loaded"][u]
    for h in range(GH):
        k, q, base = env["ks"][u][h // 2], env["qs"][u][h // 2], HALF * (h % 2)
        eng.dma_start(k[base:base + HD, :].bitcast(F32), kst[n * GH + h, 0:HD, :]).then_inc(loaded, 16)
        eng.dma_start(k[base + HD:base + R_MIX, :].bitcast(F32), kst[n * GH + h, :, :]).then_inc(loaded, 16)
        eng.dma_start(q[base:base + HD, :].bitcast(F32), qst[n * GH + h, HD:2 * HD, :]).then_inc(loaded, 16)
        eng.dma_start(q[base + HD:base + R_CUT, :].bitcast(F32), qst[n * GH + h, :, :]).then_inc(loaded, 16)
    for half in range(2):
        rows = slice(half * S // 2, (half + 1) * S // 2)
        eng.dma_start(env["vg"][u][:, half * ST // 2:(half + 1) * ST // 2, :],
                      vs[n, rows, :].rearrange("(t p) c -> p t c", p=P)).then_inc(loaded, 16)


STATS = 3


def layernorm_stats(nc, dve, x_of, st, mv, done, base):
    for t in range(NT):
        last = nc.vector.bn_stats(st[:, t, :], x_of(t))
    last.then_inc(done, 1)
    dve.wait_ge(done, base + 1)
    dve.sem_inc(done, 1)
    for t in range(NT):
        last = nc.vector.bn_aggr(mv[:, t, :], st[:, t, :])
    last.then_inc(done, 1)


def inverse_deviation(nc, pool, mv, tmp, rs, env, done, base):
    nc.gpsimd.tensor_tensor(tmp[:, :], mv[:, :, 1], env["eps"][:, :], ALU.add).then_inc(done, 1)
    pool.wait_ge(done, base + 1)
    nc.gpsimd.tensor_tensor(rs[:, :], tmp[:, :], env["neg_half"][:, :], ALU.pow).then_inc(done, 1)


def stage_projections(nc, env):
    consts, kst, qst, vs = env["consts"], env["kst"], env["qst"], env["vs"]
    x, w_kqv, m = env["x"], env["w_kqv"], env["m"]
    with ExitStack() as ctx:
        def sb(name, shape, dt=F32):
            return ctx.enter_context(nc.sbuf_tensor(f"qkv_{name}", shape, dt))

        def bank(name, shape=(P, TB)):
            return ctx.enter_context(nc.psum_tensor(f"qkv_{name}", list(shape), F32))

        def sem(name):
            return ctx.enter_context(nc.semaphore(f"qkv_{name}"))

        ident = consts[:, 0:P]
        sel = consts[:, 3 * P:3 * P + 8]
        w_raw = sb("w_raw", [P, DC, 3 * D])
        w_hi = sb("w_hi", [P, DC, 3 * D], F32R)
        w_lo = sb("w_lo", [P, DC, 3 * D], F32R)
        m_col = sb("m_col", [P, 1])
        m_hi = sb("m_hi", [P, 1], F32R)
        m_lo = sb("m_lo", [P, 1])
        m_a = sb("m_a", [P, QB])
        m_b = sb("m_b", [P, QB])
        m_wide = sb("m_wide", [P, QB, TB], F32R)
        xs = [sb(f"xs{u}", [P, NT, D]) for u in range(2)]
        xn = [sb(f"xn{u}", [P, NT, D]) for u in range(2)]
        st = [sb(f"st{u}", [P, NT, 6]) for u in range(2)]
        mv = [sb(f"mv{u}", [P, NT, 2]) for u in range(2)]
        tmp = [sb(f"tmp{u}", [P, NT]) for u in range(2)]
        rs = [sb(f"rs{u}", [P, NT]) for u in range(2)]
        xh = [sb(f"xh{u}", [P, DC, TB], F32R) for u in range(2)]
        xl = [sb(f"xl{u}", [P, DC, TB], F32R) for u in range(2)]
        kqh = [sb(f"kqh{u}", [P, 2 * DC, TB], F32R) for u in range(2)]
        kql = [sb(f"kql{u}", [P, 2 * DC, TB], F32R) for u in range(2)]
        vt = [sb(f"vt{u}", [P, NT, H, VW]) for u in range(2)]
        ps_x = [bank(f"ps_x{c}") for c in range(DC)]
        ps_kq = [bank(f"ps_kq{c}") for c in range(2 * DC)]
        ps_v = [bank(f"ps_v{c}", (P, 2, D)) for c in range(2)]

        ramp = sb("ramp", [2 * QB + 2, S])
        w_in = sem("w_in")
        ramp_in = sem("ramp_in")
        ramp_done = sem("ramp_done")
        x_in = [sem(f"x_in{u}") for u in range(2)]
        w_hi_done = sem("w_hi_done")
        w_lo_done = sem("w_lo_done")
        m_done = sem("m_done")
        m_out = sem("m_out")
        stats = sem("stats")
        rstd = sem("rstd")
        xn_done = sem("xn_done")
        x_t = sem("x_t")
        xh_done = sem("xh_done")
        xl_done = sem("xl_done")
        kq_ps = sem("kq_ps")
        kqh_done = sem("kqh_done")
        kql_done = sem("kql_done")
        v_ps = sem("v_ps")
        v_done = sem("v_done")
        v_ones = sem("v_ones")
        stored = [sem(f"stored{u}") for u in range(2)]
        out_free = sem("out_free")
        half_done = sem("half_done")
        block = ctx.enter_context(nc.Block())
        x_blocks = x.rearrange("b (i t p) d -> (b i) p t d", p=P, t=NT)
        STORES = 2 * 2 * DC + HG

        @block.sync
        def _(sp):
            sp.dma_start(consts[:, :], env["consts_in"]).then_inc(w_in, 16)
            sp.dma_start(w_raw[:, :, :], w_kqv.rearrange("(c p) n -> p c n", p=P)).then_inc(w_in, 16)
            sp.dma_start(m_col[:, :], m.rearrange("h a b -> h (a b)").unsqueeze(1).broadcast_to([H, 8, 1])).then_inc(w_in, 16)
            sp.dma_start(ramp[:, :], env["ramp_in"]).then_inc(ramp_in, 16)
            sp.sem_inc(out_free, 2)
            sp.wait_ge(ramp_done, 1)
            load_ramp(sp, env, 0)
            sp.wait_ge(m_done, 5)
            for b in range(B):
                sp.dma_start(qst[b * H:(b + 1) * H, 2 * HD:, :],
                             m_wide[:, :, :].rearrange("p i q -> p (i q)").bitcast(F32)).then_inc(m_out, 16)

            def store_batch(b):
                with sp.Fori(0, QB // 2) as ii:
                    for u in range(2):
                        g = QB * b + 2 * ii + u
                        sp.wait_ge(kql_done, 2 * DC * g + 4 * DC)
                        cols = bass.ds(ii * 2 * TB + u * TB, TB)
                        for c in range(DC):
                            heads = slice(b * H + c * (P // HD), b * H + (c + 1) * (P // HD))
                            for stack, src in ((kst, (kqh, kql)), (qst, (kql, kqh))):
                                chunk = c if stack is kst else DC + c
                                for k, part in enumerate(src):
                                    sp.dma_start(stack[heads, k * HD:(k + 1) * HD, cols],
                                                 part[u][:, chunk, :].bitcast(F32)).then_inc(stored[u], 16)
                        sp.wait_ge(v_done, 2 * g + 4)
                        for hg in range(HG):
                            dst = vs[b * HG + hg, cols, :].rearrange("(t p) c -> p t c", p=P)
                            sp.dma_start(dst, vt[u][:, :, hg * GH:(hg + 1) * GH, :].rearrange("p t h c -> p t (h c)")).then_inc(stored[u], 16)
                        sp.wait_ge(stored[u], 16 * STORES * (b * QB // 2 + ii + 1))
                        sp.sem_inc(out_free, 1)

            store_batch(0)
            sp.wait_ge(m_out, 16 * B)
            load_group(sp, env, 0, 0)
            for b in range(1, B):
                store_batch(b)

        @block.gpsimd
        def _(pool):
            nc.gpsimd.memset(env["eps"][:, :], EPS)
            nc.gpsimd.memset(env["neg_half"][:, :], -0.5).then_inc(half_done, 1)
            for u in range(2):
                pool.dma_start(xs[u][:, :, :], x_blocks[u]).then_inc(x_in[u], 16)
            pool.wait_ge(half_done, 1)

            def one(g, u, load):
                pool.wait_ge(stats, STATS * g + STATS)
                inverse_deviation(nc, pool, mv[u], tmp[u], rs[u], env, rstd, 2 * g)
                if load:
                    pool.wait_ge(xn_done, g + 1)
                    pool.dma_start(xs[u][:, :, :], x_blocks[g + 2]).then_inc(x_in[u], 16)

            with pool.Fori(0, BLOCKS // 2 - 1) as r:
                for u in range(2):
                    one(2 * r + u, u, True)
            for u in range(2):
                one(BLOCKS - 2 + u, u, False)

        @block.vector
        def _(dve):
            for u in range(2):
                last = nc.vector.memset(vt[u][:, :, :, :], 0.0)
            last.then_inc(v_ones, 1)
            dve.wait_ge(v_ones, 1)
            for u in range(2):
                last = nc.vector.memset(vt[u][:, :, :, HD:HD + 1], 1.0)
            last.then_inc(v_ones, 1)
            dve.sem_inc(xl_done, DC)
            dve.sem_inc(kql_done, 2 * DC)
            dve.wait_ge(w_in, 48)
            dve.wait_ge(w_hi_done, 1)
            nc.vector.tensor_tensor(w_lo[:, :, :], w_raw[:, :, :], w_hi[:, :, :].bitcast(F32), ALU.subtract).then_inc(w_lo_done, 1)
            nc.vector.tensor_copy(env["ident_b"][:, :], ident)
            nc.vector.tensor_copy(env["mask_kq"][:, :], consts[:, P:2 * P])
            nc.vector.tensor_copy(env["mask_qk"][:, :], consts[:, 2 * P:3 * P])
            dve.wait_ge(ramp_in, 16)
            nc.vector.tensor_copy(env["ramp_r"][:, :], ramp[:, :]).then_inc(ramp_done, 1)
            nc.vector.tensor_copy(m_hi[:, :], m_col[:, :]).then_inc(m_done, 1)
            dve.wait_ge(m_done, 1)
            nc.vector.tensor_tensor(m_lo[:, :], m_col[:, :], m_hi[:, :].bitcast(F32), ALU.subtract).then_inc(m_done, 1)
            dve.wait_ge(m_done, 2)
            nc.vector.tensor_scalar(m_a[:, :], sel[:, 0:QB], m_hi[:, :].bitcast(F32), None, ALU.mult).then_inc(m_done, 1)
            dve.wait_ge(m_done, 3)
            nc.vector.scalar_tensor_tensor(m_b[:, :], sel[:, QB:2 * QB], m_lo[:, :], m_a[:, :], ALU.mult, ALU.add).then_inc(m_done, 1)
            dve.wait_ge(m_done, 4)
            nc.vector.tensor_copy(m_wide[:, :, :], m_b[:, :].unsqueeze(2).broadcast_to([P, QB, TB])).then_inc(m_done, 1)

            def find_stats(g, u):
                dve.wait_ge(x_in[u], 8 * (g - u) + 16)
                layernorm_stats(nc, dve, lambda t: xs[u][:, t, :], st[u], mv[u], stats, STATS * g)

            def normalise(g, u):
                dve.wait_ge(rstd, 2 * g + 2)
                for t in range(NT):
                    last = nc.vector.tensor_scalar(xn[u][:, t, :], xs[u][:, t, :], mv[u][:, t, 0:1], rs[u][:, t:t + 1],
                                                   ALU.subtract, ALU.mult)
                last.then_inc(xn_done, 1)

            def x_lo(g, u):
                for c in range(DC):
                    dve.wait_ge(xh_done, DC * g + c + 1)
                    nc.vector.tensor_tensor(xl[u][:, c, :], ps_x[c][:, :], xh[u][:, c, :].bitcast(F32), ALU.subtract).then_inc(xl_done, 1)

            def kq_lo(g, u, c):
                dve.wait_ge(kqh_done, 2 * DC * g + c + 1)
                nc.vector.scalar_tensor_tensor(kql[u][:, c, :], ps_kq[c][:, :], 1.0 if c < DC else SCORE_SCALE,
                                               kqh[u][:, c, :].bitcast(F32), ALU.mult, ALU.subtract).then_inc(kql_done, 1)

            def body(g, u, more):
                if more:
                    find_stats(g + 1, 1 - u)
                dve.wait_ge(out_free, g + 1)
                kq_lo(g, u, 0)
                if more:
                    normalise(g + 1, 1 - u)
                for c in range(1, 2 * DC):
                    kq_lo(g, u, c)
                if more:
                    x_lo(g + 1, 1 - u)

            find_stats(0, 0)
            normalise(0, 0)
            x_lo(0, 0)
            with dve.Fori(0, BLOCKS // 2 - 1) as r:
                for u in range(2):
                    body(2 * r + u, u, True)
            body(BLOCKS - 2, 0, True)
            body(BLOCKS - 1, 1, False)

        @block.scalar
        def _(act):
            act.wait_ge(w_in, 48)
            nc.scalar.activation(w_hi[:, :, :], w_raw[:, :, :], ACT.Copy).then_inc(w_hi_done, 1)
            act.wait_ge(v_ones, 2)
            act.sem_inc(v_done, 2)

            def x_hi(g, u):
                for c in range(DC):
                    act.wait_ge(x_t, DC * g + c + 1)
                    nc.scalar.activation(xh[u][:, c, :], ps_x[c][:, :], ACT.Copy).then_inc(xh_done, 1)

            def body(g, u, more):
                act.wait_ge(out_free, g + 1)
                for c in range(2 * DC):
                    act.wait_ge(kq_ps, 2 * DC * g + c + 1)
                    nc.scalar.activation(kqh[u][:, c, :], ps_kq[c][:, :], ACT.Copy,
                                         scale=1.0 if c < DC else SCORE_SCALE).then_inc(kqh_done, 1)
                if more:
                    x_hi(g + 1, 1 - u)
                for v in range(2):
                    act.wait_ge(v_ps, 2 * g + v + 1)
                    nc.scalar.activation(vt[u][:, 2 * v:2 * v + 2, :, 0:HD],
                                         ps_v[v][:, :, :].rearrange("p t (h d) -> p t h d", d=HD), ACT.Copy).then_inc(v_done, 1)

            x_hi(0, 0)
            with act.Fori(0, BLOCKS // 2 - 1) as r:
                for u in range(2):
                    body(2 * r + u, u, True)
            body(BLOCKS - 2, 0, True)
            body(BLOCKS - 1, 1, False)

        @block.tensor
        def _(pe):
            def turn(g, u):
                pe.wait_ge(xn_done, g + 1)
                for c in range(DC):
                    pe.wait_ge(xl_done, DC * g + c + 1)
                    for t in range(NT):
                        last = nc.tensor.transpose(ps_x[c][:, t * P:(t + 1) * P], xn[u][:, t, c * P:(c + 1) * P], ident)
                    last.then_inc(x_t, 1)

            def body(g, u, more):
                pe.wait_ge(xl_done, DC * g + 2 * DC)
                for c in range(2 * DC):
                    pe.wait_ge(kql_done, 2 * DC * g + c + 1)
                    n = 0
                    for k in range(DC):
                        for w, xx in ((w_hi, xh), (w_hi, xl), (w_lo, xh)):
                            last = nc.tensor.matmul(ps_kq[c][:, :], w[:, k, c * P:(c + 1) * P], xx[u][:, k, :],
                                                    start=(n == 0), stop=(n == 3 * DC - 1))
                            n += 1
                    last.then_inc(kq_ps, 1)
                if more:
                    turn(g + 1, 1 - u)
                for v in range(2):
                    pe.wait_ge(v_done, 2 * g + v + 1)
                    for j in range(2):
                        n = 0
                        for k in range(DC):
                            for w, xx in ((w_hi, xh), (w_hi, xl), (w_lo, xh)):
                                last = nc.tensor.matmul(ps_v[v][:, j, :], xx[u][:, k, (2 * v + j) * P:(2 * v + j + 1) * P],
                                                        w[:, k, 2 * D:3 * D], start=(n == 0), stop=(n == 3 * DC - 1))
                                n += 1
                    last.then_inc(v_ps, 1)

            turn(0, 0)
            pe.wait_ge(w_lo_done, 1)
            with pe.Fori(0, BLOCKS // 2 - 1) as r:
                for u in range(2):
                    body(2 * r + u, u, True)
            body(BLOCKS - 2, 0, True)
            body(BLOCKS - 1, 1, False)


MAX_UNITS = [(t, p, c, e) for t in range(ST) for p in range(GH // 2) for c in range(t // NT + 1) for e in range(2)]
STEPS = [(i, j) for i in range(QB) for j in range(NT * (i + 1))]
PER_STEP = len(MAX_UNITS) // len(STEPS)
LEAD = 80
RING = 3
P_SLOTS = 4
CUTS = 2 * GH


def first_step(i):
    return NT * i * (i + 1) // 2


def max_events(first, last):
    ends = [sum(GH * NT * (i + 1) for i in range(b + 1)) for b in range(QB)]
    out = []
    for at in range(first, last, PER_STEP):
        events = []
        for k in range(at, at + PER_STEP):
            events.append(("max", MAX_UNITS[k]))
            if k + 1 in ends:
                events.append(("finish", ends.index(k + 1)))
        if at in ends:
            events.append(("cut", ends.index(at)))
        out.append(events)
    return out


def prologue_schedule():
    return [(what, arg, 0) for events in max_events(0, LEAD) for what, arg in events]


def group_schedule(more):
    own, ahead = max_events(LEAD, len(MAX_UNITS)), max_events(0, LEAD)
    out = []
    for s, (i, j) in enumerate(STEPS):
        out.append(("scores", s, 0))
        if s < len(own):
            out += [(what, arg, 0) for what, arg in own[s]]
        else:
            if s == len(own):
                out.append(("cut", QB - 1, 0))
            if more:
                out += [(what, arg, 1) for what, arg in ahead[s - len(own)]]
        if s:
            if s - 1 == first_step(STEPS[s - 1][0]) and s > 1:
                out.append(("turn", STEPS[s - 1][0] - 1, 0))
            out.append(("values", s - 1, 0))
    return out + [("values", len(STEPS) - 1, 0), ("turn", QB - 1, 0)]


def ring_events(schedule):
    return [x for x in schedule if x[0] in ("max", "cut", "turn")]


UNITS_PROLOGUE = len(ring_events(prologue_schedule()))
UNITS_GROUP = len(ring_events(group_schedule(True)))
RING_START = RING + (-UNITS_PROLOGUE) % RING
assert UNITS_GROUP % RING == 0 and LEAD + len(STEPS) * PER_STEP == len(MAX_UNITS) + LEAD


def q_of(n):
    return RING_START + UNITS_PROLOGUE + UNITS_GROUP * n


def stage_attention(nc, env):
    att, loaded, ramp_set = env["att"], env["loaded"], env["ramp_set"]
    with ExitStack() as ctx:
        def sb(name, shape, dt=F32):
            return ctx.enter_context(nc.sbuf_tensor(f"att_{name}", shape, dt))

        def bank(name, shape=(P, TB)):
            return ctx.enter_context(nc.psum_tensor(f"att_{name}", list(shape), F32))

        def sem(name):
            return ctx.enter_context(nc.semaphore(f"att_{name}"))

        ident = env["consts"][:, 0:P]
        for name, shape, dt in (("ks", [P, S], F32R), ("qs", [P, S], F32R)):
            env[name].append([sb(f"{name}1{p}", shape, dt) for p in range(2)])
        env["vg"].append(sb("vg1", [P, ST, GH * VW]))
        ks, qs, vg = env["ks"], env["qs"], env["vg"]
        probs = [sb(f"probs{n}", [P, GH, TB]) for n in range(P_SLOTS)]
        part_max = sb("part_max", [P, GH, ST, QB])
        neg_max = [sb(f"neg_max{n}", [P, P // NT, NT]) for n in range(2)]
        cut_hi = [sb(f"cut_hi{n}", [GH * NT, P], F32R) for n in range(2)]
        cut_lo = [sb(f"cut_lo{n}", [GH * NT, P], F32R) for n in range(2)]
        o_t = sb("o_t", [P, TB])
        inv = sb("inv", [P, NT * GH])
        ps_s = [bank(f"ps_s{p}", (P, 2, TB)) for p in range(2)]
        ring = [bank(f"ring{n}") for n in range(RING)]
        ps_o = bank("ps_o")

        cut_set = sem("cut_set")
        scores_ps = sem("scores_ps")
        exp_done = sem("exp_done")
        pv_done = sem("pv_done")
        o_copied = sem("o_copied")
        ring_ps = sem("ring_ps")
        ring_used = sem("ring_used")
        max_done = sem("max_done")
        cut_part = sem("cut_part")
        inv_done = sem("inv_done")
        block = ctx.enter_context(nc.Block())

        @block.sync
        def _(sp):
            load_ramp(sp, env, 1)

            def cuts(schedule, q0, n, u):
                for k, (what, i, ahead) in enumerate(ring_events(schedule)):
                    if what != "cut":
                        continue
                    w = QB * (n + ahead) + i
                    sp.wait_ge(ring_used, q0 + k + 1)
                    if not (isinstance(w, int) and w == 0):
                        sp.wait_ge(cut_set, 16 * CUTS * w)
                    for h in range(GH):
                        p, base = h // 2, HALF * (h % 2)
                        for r, src in enumerate((cut_hi, cut_lo)):
                            row = base + R_CUT + r
                            sp.dma_start(qs[(u + ahead) % 2][p][row:row + 1, i * TB:(i + 1) * TB].bitcast(F32),
                                         src[i % 2][h * NT:(h + 1) * NT, :].bitcast(F32)).then_inc(cut_set, 16)

            cuts(prologue_schedule(), RING_START, 0, 0)
            with sp.Fori(0, GROUPS // 2 - 1) as r:
                for u in range(2):
                    cuts(group_schedule(True), q_of(2 * r + u), 2 * r + u, u)
            cuts(group_schedule(True), q_of(GROUPS - 2), GROUPS - 2, 0)
            cuts(group_schedule(False), q_of(GROUPS - 1), GROUPS - 1, 1)

        @block.scalar
        def _(act):
            act.sem_inc(exp_done, 2)
            act.sem_inc(o_copied, 1)

            def group(n, u, more):
                for s, (i, j) in enumerate(STEPS):
                    if s == 1 and more:
                        act.wait_ge(pv_done, len(STEPS) * n + P_SLOTS)
                        load_group(act, env, n + 1, 1 - u)
                    skip = max(0, (j - NT * i) * P)
                    for p in range(2):
                        act.wait_ge(scores_ps, 2 * len(STEPS) * n + 2 * s + p + 1)
                        if p == 0:
                            act.wait_ge(pv_done, len(STEPS) * n + s + 1)
                        nc.scalar.activation(probs[s % P_SLOTS][:, 2 * p:2 * p + 2, skip:TB], ps_s[p][:, :, skip:TB],
                                             ACT.Exp).then_inc(exp_done, 1)
                    if s == first_step(i) and i > 0:
                        copy_out(n, i - 1)
                copy_out(n, QB - 1)

            def copy_out(n, i):
                last_step = first_step(i + 1) - 1
                act.wait_ge(pv_done, len(STEPS) * n + last_step + 1 + P_SLOTS)
                nc.scalar.activation(o_t[:, :], ps_o[:, :], ACT.Copy).then_inc(o_copied, 1)

            with act.Fori(0, GROUPS // 2 - 1) as r:
                for u in range(2):
                    group(2 * r + u, u, True)
            group(GROUPS - 2, 0, True)
            group(GROUPS - 1, 1, False)

        @block.vector
        def _(dve):
            dve.sem_inc(ring_used, RING_START)
            for n in range(2):
                nc.vector.memset(neg_max[n][:, GH:, :], 0.0)

            def run(schedule, q0, bank0, n, u):
                q = k = 0
                for what, arg, ahead in schedule:
                    if what in ("scores", "values"):
                        continue
                    q, bank = q0 + k, (bank0 + k) % RING
                    if what == "finish":
                        dve.wait_ge(ring_used, q)
                        nc.vector.tensor_reduce(neg_max[arg % 2][:, 0:GH, :], part_max[:, :, NT * arg:NT * (arg + 1), 0:arg + 1],
                                                op=ALU.max, axis=AX.X, negate=True).then_inc(max_done, 1)
                        continue
                    dve.wait_ge(ring_ps, q + 1)
                    if what == "max":
                        t, p, c, e = arg
                        w = P * (t % NT + 1) if c == t // NT else TB
                        nc.vector.reduce_max(part_max[:, 2 * p + e, t, c:c + 1], ring[bank][:, 0:w], axis=AX.X).then_inc(ring_used, 1)
                    elif what == "cut":
                        nc.vector.tensor_copy(cut_hi[arg % 2][:, :], ring[bank][0:GH * NT, 0:P]).then_inc(cut_part, 1)
                        dve.wait_ge(cut_part, QB * (n + ahead) + arg + 1)
                        nc.vector.tensor_tensor(cut_lo[arg % 2][:, :], ring[bank][0:GH * NT, 0:P], cut_hi[arg % 2][:, :].bitcast(F32),
                                                ALU.subtract).then_inc(ring_used, 1)
                    else:
                        o = ring[bank][:, :].rearrange("p (g c) -> p g c", c=VW)
                        dve.wait_ge(ring_used, q)
                        nc.vector.reciprocal(inv[:, :], o[:, :, HD]).then_inc(inv_done, 1)
                        dve.wait_ge(inv_done, QB * n + arg + 1)
                        dst = att[:, bass.ds(n // HG * ST + NT * arg, NT), bass.ds(n % HG * (GH * HD), GH * HD)].rearrange("p t (h d) -> p t h d", d=HD)
                        nc.vector.tensor_tensor(dst, o[:, :, 0:HD].rearrange("p (t h) d -> p t h d", h=GH),
                                                inv[:, :].rearrange("p (t h) -> p t h", h=GH).unsqueeze(3).broadcast_to([P, NT, GH, HD]),
                                                ALU.mult).then_inc(ring_used, 1)
                    k += 1

            run(prologue_schedule(), RING_START, RING_START % RING, 0, 0)
            with dve.Fori(0, GROUPS // 2 - 1) as r:
                for u in range(2):
                    run(group_schedule(True), q_of(2 * r + u), 0, 2 * r + u, u)
            run(group_schedule(True), q_of(GROUPS - 2), 0, GROUPS - 2, 0)
            run(group_schedule(False), q_of(GROUPS - 1), 0, GROUPS - 1, 1)

        @block.tensor
        def _(pe):
            pe.sem_inc(pv_done, P_SLOTS)

            def scores(n, u, s):
                i, j = STEPS[s]
                if j == 0:
                    pe.wait_ge(cut_set, 16 * CUTS * (QB * n + i + 1))
                skip = max(0, (j - NT * i) * P)
                for p in range(2):
                    pe.wait_ge(exp_done, 2 * len(STEPS) * n + 2 * s + p + 1)
                    for e in range(2):
                        rows = slice(HALF * e, HALF * e + R_ALL)
                        last = nc.tensor.matmul(ps_s[p][:, e, skip:TB], ks[u][p][rows, j * P:(j + 1) * P],
                                                qs[u][p][rows, i * TB + skip:(i + 1) * TB], start=True, stop=j < NT * i)
                    if j >= NT * i:
                        for e in range(2):
                            last = nc.tensor.matmul(ps_s[p][:, e, skip:skip + P], env["ident_b"][:, :], env["mask_kq"][:, :],
                                                    start=False, stop=True)
                    last.then_inc(scores_ps, 1)

            def values(n, u, s):
                i, j = STEPS[s]
                skip = max(0, (j - NT * i) * P)
                pe.wait_ge(exp_done, 2 * len(STEPS) * n + 2 * s + 2 + 2)
                if j == 0:
                    pe.wait_ge(o_copied, QB * n + i + 1)
                for h in range(GH):
                    last = nc.tensor.matmul(ps_o[VW * h:VW * (h + 1), skip:TB], vg[u][:, j, VW * h:VW * (h + 1)],
                                            probs[s % P_SLOTS][:, h, skip:TB], start=(j == 0), stop=(j == NT * (i + 1) - 1))
                last.then_inc(pv_done, 1)

            def run(schedule, q0, bank0, n, u):
                k = 0
                for what, arg, ahead in schedule:
                    if what == "scores":
                        scores(n, u, arg)
                    elif what == "values":
                        values(n, u, arg)
                    elif what != "finish":
                        pe.wait_ge(ring_used, q0 + k - RING + 1)
                        if what == "max":
                            if arg == MAX_UNITS[0] and ahead:
                                pe.wait_ge(ramp_set[1 - u], 16 * RAMPS)
                                pe.wait_ge(loaded[1 - u], load_count(n + 1, 1 - u))
                            last = max_unit(ring[(bank0 + k) % RING], arg, (u + ahead) % 2)
                        elif what == "cut":
                            pe.wait_ge(max_done, QB * (n + ahead) + arg + 1)
                            last = nc.tensor.transpose(ring[(bank0 + k) % RING][:, 0:P], neg_max[arg % 2][:, :, :].rearrange("p h t -> p (h t)"), ident)
                        else:
                            pe.wait_ge(o_copied, QB * n + arg + 2)
                            for t in range(NT):
                                last = nc.tensor.transpose(ring[(bank0 + k) % RING][:, t * P:(t + 1) * P], o_t[:, t * P:(t + 1) * P], ident)
                        last.then_inc(ring_ps, 1)
                        k += 1

            def max_unit(bank, arg, u):
                t, p, c, e = arg
                diagonal = c == t // NT
                w = P * (t % NT + 1) if diagonal else TB
                rows = slice(HALF * e, HALF * e + R_CUT)
                last = nc.tensor.matmul(bank[:, 0:w], qs[u][p][rows, t * P:(t + 1) * P],
                                        ks[u][p][rows, c * TB:c * TB + w], start=True, stop=not diagonal)
                if diagonal:
                    last = nc.tensor.matmul(bank[:, w - P:w], env["ident_b"][:, :], env["mask_qk"][:, :], start=False, stop=True)
                return last

            def load_count(n, u):
                return 8 * LOADS * (n - u) + 16 * LOADS

            pe.sem_inc(ring_ps, RING_START)
            pe.wait_ge(ramp_set[0], 16 * RAMPS)
            pe.wait_ge(loaded[0], 16 * LOADS)
            run(prologue_schedule(), RING_START, RING_START % RING, 0, 0)
            with pe.Fori(0, GROUPS // 2 - 1) as r:
                for u in range(2):
                    run(group_schedule(True), q_of(2 * r + u), 0, 2 * r + u, u)
            run(group_schedule(True), q_of(GROUPS - 2), 0, GROUPS - 2, 0)
            run(group_schedule(False), q_of(GROUPS - 1), 0, GROUPS - 1, 1)


W_PIECE = HID


def weight_piece(src, hi, lo, o, n):
    chunks = src.shape[0] // P
    assert chunks * n == W_PIECE
    return src.rearrange("(c p) n -> p c n", p=P)[:, :, o:o + n], hi[:, :, o:o + n], lo[:, :, o:o + n], chunks


def staged(stage, n, chunks):
    return stage[n % 2][:, :].rearrange("p (c n) -> p c n", c=chunks)


def load_pieces(sp, pieces, stage, w_in, w_lo_done):
    for n, (src, _, _, chunks) in enumerate(pieces):
        if n >= 2:
            sp.wait_ge(w_lo_done, n - 1)
        sp.dma_start(staged(stage, n, chunks), src).then_inc(w_in[n % 2], 16)


def piece_hi(nc, act, pieces, stage, n, w_in, w_hi_done):
    _, hi, _, chunks = pieces[n]
    act.wait_ge(w_in[n % 2], 16 * (n // 2 + 1))
    nc.scalar.activation(hi, staged(stage, n, chunks), ACT.Copy).then_inc(w_hi_done, 1)


def piece_lo(nc, dve, pieces, stage, n, w_hi_done, w_lo_done):
    _, hi, lo, chunks = pieces[n]
    dve.wait_ge(w_hi_done, n + 1)
    nc.vector.tensor_tensor(lo, staged(stage, n, chunks), hi.bitcast(F32), ALU.subtract).then_inc(w_lo_done, 1)


def largest_low_part(nc, dve, lows, w_lo_done, pieces, low_max, done):
    dve.wait_ge(w_lo_done, len(pieces))
    for k, low in enumerate(lows):
        last = nc.vector.tensor_reduce(low_max[:, k:k + 1], low[:, :, :].bitcast(F32), op=ALU.max, axis=AX.XY, apply_absolute_value=True)
    last.then_inc(done, 1)
    dve.wait_ge(done, 1)
    nc.vector.reduce_max(low_max[:, len(lows):len(lows) + 1], low_max[:, 0:len(lows)], axis=AX.X).then_inc(done, 1)


def low_over_partitions(nc, pool, low_max, low_all, done, all_done):
    n = low_max.shape[1] - 1
    pool.wait_ge(done, 2)
    nc.gpsimd.partition_all_reduce(low_all[:, :], low_max[:, n:n + 1], P, RMAX).then_inc(all_done, 1)


def by_weights(pe, low_all, all_done, blocks):
    pe.wait_ge(all_done, 1)
    bits = pe.value_load(low_all[0:1, 0:1].bitcast(mybir.dt.int32), min_val=0, max_val=2 ** 31 - 1)
    with pe.If(bits == 0):
        blocks(True)
    with pe.Else():
        blocks(False)


def passes(w_hi, w_lo, x_hi, x_lo, exact):
    return ((w_hi, x_hi), (w_hi, x_lo)) if exact else ((w_hi, x_hi), (w_hi, x_lo), (w_lo, x_hi))


def dense_512(nc, out, w_hi, w_lo, x_hi, x_lo, chunks, o, exact, ready=None):
    pairs = passes(w_hi, w_lo, x_hi, x_lo, exact)
    n = 0
    for c in range(chunks):
        if ready:
            ready(c)
        for w, xx in pairs:
            last = nc.tensor.matmul(out, w[:, c, o * P:(o + 1) * P], xx[:, c, :], start=(n == 0), stop=(n == len(pairs) * chunks - 1))
            n += 1
    return last


def stage_ffn_in(nc, env):
    x, att, x1, h2 = env["x"], env["att"], env["x1"], env["h2"]
    with ExitStack() as ctx:
        def sb(name, shape, dt=F32):
            return ctx.enter_context(nc.sbuf_tensor(f"fin_{name}", shape, dt))

        def bank(name, shape=(P, TB)):
            return ctx.enter_context(nc.psum_tensor(f"fin_{name}", list(shape), F32))

        def sem(name):
            return ctx.enter_context(nc.semaphore(f"fin_{name}"))

        ident = env["consts"][:, 0:P]
        w1h, w1l, w2h, w2l = (sb(n, [P, DC, HID], F32R) for n in ("w1h", "w1l", "w2h", "w2l"))
        h1h, h1l = (sb(n, [P, HC, HID], F32R) for n in ("h1h", "h1l"))
        scales = sb("scales", [P, 4, HC])
        xs = sb("xs", [P, NT, D])
        xo = sb("xo", [P, NT, D])
        xn = sb("xn", [P, NT, D])
        st, mv, tmp, rs = sb("st", [P, NT, 6]), sb("mv", [P, NT, 2]), sb("tmp", [P, NT]), sb("rs", [P, NT])
        xh, xl = sb("xh", [P, DC, TB], F32R), sb("xl", [P, DC, TB], F32R)
        gate = [sb(f"gate{n}", [P, TB]) for n in range(2)]
        hf = [sb(f"hf{n}", [P, TB]) for n in range(2)]
        hh, hl = sb("hh", [P, HC, TB], F32R), sb("hl", [P, HC, TB], F32R)
        HALFC = HC // 2
        ho = sb("ho", [P, HALFC, TB])
        low_max, low_all = sb("low_max", [P, 4]), sb("low_all", [P, 1])
        ps_x = [bank(f"ps_x{c}") for c in range(DC)]
        ps_1 = [bank(f"ps_1{n}", (P, 2, TB)) for n in range(2)]
        ps_2 = [bank(f"ps_2{n}") for n in range(2)]

        w_in = [sem(f"w_in{n}") for n in range(2)]
        names = ("w_hi_done w_lo_done s_in x_in stats rstd a_done x1_done xn_done x1_out x_t xh_done xl_done l1_ps gate_done "
                 "hf_done hh_done hl_done l2_ps gelu_done h2_out h2_free low_done low_all_done")
        (w_hi_done, w_lo_done, s_in, x_in, stats, rstd, a_done, x1_done, xn_done, x1_out, x_t, xh_done, xl_done, l1_ps, gate_done,
         hf_done, hh_done, hl_done, l2_ps, gelu_done, h2_out, h2_free, low_done, low_all_done) = (sem(n) for n in names.split())
        stage = [sb(f"stage{n}", [P, W_PIECE]) for n in range(2)]
        WIDE = W_PIECE // DC
        pieces = []
        for o in range(0, HID, WIDE):
            pieces += [weight_piece(env["w1"], w1h, w1l, o, WIDE), weight_piece(env["w2"], w2h, w2l, o, WIDE)]
        LAYER1_PIECES = len(pieces)
        pieces += [weight_piece(env["h1"], h1h, h1l, o * P, P) for o in range(HC)]
        block = ctx.enter_context(nc.Block())
        x_blocks = x.rearrange("b (i t p) d -> (b i) p t d", p=P, t=NT)
        LAST = BLOCKS - 1

        @block.sync
        def _(sp):
            sp.dma_start(scales[:, :, :], env["scales"]).then_inc(s_in, 16)
            sp.dma_start(xs[:, :, :], x_blocks[0]).then_inc(x_in, 16)
            load_pieces(sp, pieces, stage, w_in, w_lo_done)
            sp.sem_inc(h2_free, 1)
            sp.wait_ge(x1_done, 1)
            sp.dma_start(x1[0], xo[:, :, :]).then_inc(x1_out, 16)
            sp.dma_start(xs[:, :, :], x_blocks[1]).then_inc(x_in, 16)

            def body(g, last):
                if not last:
                    sp.wait_ge(x1_done, g + 2)
                    sp.dma_start(x1[g + 1], xo[:, :, :]).then_inc(x1_out, 16)
                for k in range(2):
                    sp.wait_ge(gelu_done, HC * g + HALFC * (k + 1) + 2)
                    sp.dma_start(h2[g, :, HALFC * k:HALFC * (k + 1), :], ho[:, :, :]).then_inc(h2_out, 16)
                    sp.wait_ge(h2_out, 32 * g + 16 * (k + 1))
                    sp.sem_inc(h2_free, 1)

            with sp.Fori(0, LAST - 1) as g:
                sp.wait_ge(x1_done, g + 2)
                sp.dma_start(xs[:, :, :], x_blocks[g + 2]).then_inc(x_in, 16)
                body(g, False)
            body(LAST - 1, False)
            body(LAST, True)
            sp.wait_ge(x1_out, 16 * BLOCKS)

        @block.gpsimd
        def _(pool):
            def deviations(first, last):
                with pool.Fori(first, last) as k:
                    pool.wait_ge(stats, STATS * k + STATS)
                    inverse_deviation(nc, pool, mv, tmp, rs, env, rstd, 2 * k)

            deviations(0, 4)
            low_over_partitions(nc, pool, low_max, low_all, low_done, low_all_done)
            deviations(4, 2 * BLOCKS)

        @block.scalar
        def _(act):
            act.wait_ge(s_in, 16)
            act.sem_inc(gelu_done, 2)

            def x_parts(g):
                for c in range(DC):
                    act.wait_ge(x_t, DC * g + c + 1)
                    nc.scalar.activation(xh[:, c, :], ps_x[c][:, :], ACT.Copy).then_inc(xh_done, 1)

            def hidden_hi(g, o):
                act.wait_ge(hf_done, HC * g + o + 3)
                nc.scalar.activation(hh[:, o, :], hf[o % 2][:, :], ACT.Copy).then_inc(hh_done, 1)

            def body(g, last, first=False):
                for o in range(HC):
                    act.wait_ge(l1_ps, HC * g + o + 1)
                    nc.scalar.activation(gate[o % 2][:, :], ps_1[o % 2][:, 0, :], ACT.Silu, scale=scales[:, 0, o:o + 1]).then_inc(gate_done, 1)
                    if o:
                        hidden_hi(g, o - 1)
                    if first:
                        piece_hi(nc, act, pieces, stage, LAYER1_PIECES + o, w_in, w_hi_done)
                hidden_hi(g, HC - 1)
                for o in range(HC):
                    if o % HALFC == 0:
                        act.wait_ge(h2_free, 2 * g + o // HALFC + 1)
                    act.wait_ge(l2_ps, HC * g + o + 1)
                    nc.scalar.activation(ho[:, o % HALFC, :], ps_2[o % 2][:, :], ACT.Gelu, scale=scales[:, 2, o:o + 1]).then_inc(gelu_done, 1)
                    if o == HALFC - 1 and not last:
                        x_parts(g + 1)

            for n in range(LAYER1_PIECES):
                piece_hi(nc, act, pieces, stage, n, w_in, w_hi_done)
            x_parts(0)
            body(0, False, first=True)
            with act.Fori(1, LAST) as g:
                body(g, False)
            body(LAST, True)

        @block.vector
        def _(dve):
            dve.sem_inc(hf_done, 2)
            dve.sem_inc(hl_done, 2)

            def prepare(g, first=False):
                a = att[:, bass.ds(g * NT, NT), :]
                dve.wait_ge(x_in, 16 * g + 16)
                layernorm_stats(nc, dve, lambda t: a[:, t, :], st, mv, stats, 2 * STATS * g)
                dve.wait_ge(rstd, 4 * g + 2)
                for t in range(NT):
                    last = nc.vector.tensor_scalar(xn[:, t, :], a[:, t, :],
                                                   mv[:, t, 0:1], rs[:, t:t + 1], ALU.subtract, ALU.mult)
                last.then_inc(a_done, 1)
                dve.wait_ge(a_done, g + 1)
                if not first:
                    dve.wait_ge(x1_out, 16 * g)
                nc.vector.tensor_tensor(xo[:, :, :], xn[:, :, :], xs[:, :, :], ALU.add).then_inc(x1_done, 1)
                dve.wait_ge(x1_done, g + 1)
                layernorm_stats(nc, dve, lambda t: xo[:, t, :], st, mv, stats, 2 * STATS * g + STATS)
                dve.wait_ge(rstd, 4 * g + 4)
                for t in range(NT):
                    last = nc.vector.tensor_scalar(xn[:, t, :], xo[:, t, :], mv[:, t, 0:1], rs[:, t:t + 1], ALU.subtract, ALU.mult)
                last.then_inc(xn_done, 1)

            def x_parts(g):
                for c in range(DC):
                    dve.wait_ge(xh_done, DC * g + c + 1)
                    nc.vector.tensor_tensor(xl[:, c, :], ps_x[c][:, :], xh[:, c, :].bitcast(F32), ALU.subtract).then_inc(xl_done, 1)

            def hidden_lo(g, o):
                dve.wait_ge(hh_done, HC * g + o + 1)
                nc.vector.tensor_tensor(hl[:, o, :], hf[o % 2][:, :], hh[:, o, :].bitcast(F32), ALU.subtract).then_inc(hl_done, 1)

            def layer1(g, first=False):
                for o in range(HC):
                    dve.wait_ge(gate_done, HC * g + o + 1)
                    dve.wait_ge(hl_done, HC * g + o + 1)
                    nc.vector.scalar_tensor_tensor(hf[o % 2][:, :], ps_1[o % 2][:, 1, :], scales[:, 1, o:o + 1], gate[o % 2][:, :],
                                                   ALU.mult, ALU.mult).then_inc(hf_done, 1)
                    if o:
                        hidden_lo(g, o - 1)
                    if first:
                        piece_lo(nc, dve, pieces, stage, LAYER1_PIECES + o, w_hi_done, w_lo_done)
                hidden_lo(g, HC - 1)

            prepare(0, first=True)
            for n in range(LAYER1_PIECES):
                piece_lo(nc, dve, pieces, stage, n, w_hi_done, w_lo_done)
            x_parts(0)
            layer1(0, first=True)
            prepare(1)
            x_parts(1)
            largest_low_part(nc, dve, (w1l, w2l, h1l), w_lo_done, pieces, low_max, low_done)
            with dve.Fori(1, LAST) as g:
                layer1(g)
                prepare(g + 1)
                x_parts(g + 1)
            layer1(LAST)

        @block.tensor
        def _(pe):
            def turn(g):
                pe.wait_ge(xn_done, g + 1)
                for c in range(DC):
                    for t in range(NT):
                        last = nc.tensor.transpose(ps_x[c][:, t * P:(t + 1) * P], xn[:, t, c * P:(c + 1) * P], ident)
                    last.then_inc(x_t, 1)

            def body(g, last_block, exact):
                pe.wait_ge(xh_done, DC * g + DC)
                pe.wait_ge(xl_done, DC * g + DC)
                for o in range(HC):
                    pe.wait_ge(w_lo_done, 2 * (o * P // WIDE) + 2)
                    pe.wait_ge(hf_done, HC * g + o + 1)
                    dense_512(nc, ps_1[o % 2][:, 0, :], w1h, w1l, xh, xl, DC, o, exact)
                    dense_512(nc, ps_1[o % 2][:, 1, :], w2h, w2l, xh, xl, DC, o, exact).then_inc(l1_ps, 1)
                for o in range(HC):
                    pe.wait_ge(w_lo_done, LAYER1_PIECES + o + 1)
                    pe.wait_ge(gelu_done, HC * g + o + 1)
                    dense_512(nc, ps_2[o % 2][:, :], h1h, h1l, hh, hl, HC, o, exact,
                              ready=(lambda c: pe.wait_ge(hl_done, HC * g + c + 3)) if o == 0 else None).then_inc(l2_ps, 1)
                    if o == HALFC - 1 and not last_block:
                        turn(g + 1)

            def blocks(exact):
                with pe.Fori(1, LAST) as g:
                    body(g, False, exact)
                body(LAST, True, exact)

            turn(0)
            body(0, False, False)
            by_weights(pe, low_all, low_all_done, blocks)


def stage_ffn_out(nc, env):
    x1, h2, out = env["x1"], env["h2"], env["out"]
    with ExitStack() as ctx:
        def sb(name, shape, dt=F32):
            return ctx.enter_context(nc.sbuf_tensor(f"fout_{name}", shape, dt))

        def bank(name, shape=(P, TB)):
            return ctx.enter_context(nc.psum_tensor(f"fout_{name}", list(shape), F32))

        def sem(name):
            return ctx.enter_context(nc.semaphore(f"fout_{name}"))

        h2h, h2l = (sb(n, [P, HC, HID], F32R) for n in ("h2h", "h2l"))
        w3h, w3l = (sb(n, [P, HC, D], F32R) for n in ("w3h", "w3l"))
        scales = sb("scales2", [P, HC])
        s3 = sb("s3", [P, D])
        hin = sb("hin", [P, HC, TB])
        ah, al = sb("ah", [P, HC, TB], F32R), sb("al", [P, HC, TB], F32R)
        hf = [sb(f"hg{n}", [P, TB]) for n in range(2)]
        bh, bl = sb("bh", [P, HC, TB], F32R), sb("bl", [P, HC, TB], F32R)
        xr = sb("xr", [P, NT, D])
        y = sb("y", [P, NT, D])
        yo = sb("yo", [P, NT, D])
        low_max, low_all = sb("low_max", [P, 3]), sb("low_all", [P, 1])
        st, mv, tmp, rs = sb("st", [P, NT, 6]), sb("mv", [P, NT, 2]), sb("tmp", [P, NT]), sb("rs", [P, NT])
        ps_3 = [bank(f"ps_3{n}") for n in range(4)]
        ps_y = [bank(f"ps_y{n}") for n in range(4)]
        w_in = [sem(f"v_in{n}") for n in range(2)]
        names = ("w_hi_done2 w_lo_done2 s_in2 h_in x_in2 stats2 rstd2 ah_done al_done l3_ps gelu_done2 bh_done bl_done "
                 "y_ps y_done n_done o_done out_done low_done2 low_all_done2")
        (w_hi_done, w_lo_done, s_in, h_in, x_in, stats, rstd, ah_done, al_done, l3_ps, gelu_done, bh_done, bl_done,
         y_ps, y_done, n_done, o_done, out_done, low_done, low_all_done) = (sem(n) for n in names.split())
        stage = [sb(f"stage{n}", [P, W_PIECE]) for n in range(2)]
        h_first = [sem(f"h_first{n}") for n in range(HC // 2)]
        pieces = [weight_piece(env["h2w"], h2h, h2l, o * P, P) for o in range(HC)]
        pieces += [weight_piece(env["w3"], w3h, w3l, o * P, P) for o in range(DC)]
        block = ctx.enter_context(nc.Block())
        LAST = BLOCKS - 1
        out_blocks = out.rearrange("b (i t p) d -> (b i) p t d", p=P, t=NT)

        @block.sync
        def _(sp):
            sp.dma_start(scales[:, :], env["scales"][:, 3, :]).then_inc(s_in, 16)
            sp.dma_start(s3[:, :], env["s3"].partition_broadcast(P)).then_inc(s_in, 16)
            for c in range(0, HC, 2):
                sp.dma_start(hin[:, c:c + 2, :], h2[0, :, c:c + 2, :]).then_inc(h_first[c // 2], 16)
            load_pieces(sp, pieces, stage, w_in, w_lo_done)
            sp.dma_start(xr[:, :, :], x1[0]).then_inc(x_in, 16)

            def body(g, last):
                if not last:
                    sp.wait_ge(al_done, HC // 2 * g + HC // 2)
                    sp.dma_start(hin[:, :, :], h2[g + 1]).then_inc(h_in, 16)
                sp.wait_ge(o_done, g + 1)
                sp.dma_start(out_blocks[g], yo[:, :, :]).then_inc(out_done, 16)
                if not last:
                    sp.dma_start(xr[:, :, :], x1[g + 1]).then_inc(x_in, 16)

            with sp.Fori(0, LAST) as g:
                body(g, False)
            body(LAST, True)
            sp.wait_ge(out_done, 16 * BLOCKS)

        @block.gpsimd
        def _(pool):
            low_over_partitions(nc, pool, low_max, low_all, low_done, low_all_done)
            with pool.Fori(0, BLOCKS) as k:
                pool.wait_ge(stats, STATS * k + STATS)
                inverse_deviation(nc, pool, mv, tmp, rs, env, rstd, 2 * k)

        @block.scalar
        def _(act):
            act.wait_ge(s_in, 32)
            act.sem_inc(gelu_done, 4)

            def split(g, first=False):
                if not first:
                    act.wait_ge(h_in, 16 * g)
                for c in range(0, HC, 2):
                    if first:
                        act.wait_ge(h_first[c // 2], 16)
                    nc.scalar.activation(ah[:, c:c + 2, :], hin[:, c:c + 2, :], ACT.Copy).then_inc(ah_done, 1)

            def body(g, last, first=False):
                for o in range(HC):
                    if first:
                        piece_hi(nc, act, pieces, stage, o + 1, w_in, w_hi_done)
                    act.wait_ge(l3_ps, HC * g + o + 1)
                    act.wait_ge(bl_done, HC * g + o + 1)
                    nc.scalar.activation(hf[o % 2][:, :], ps_3[o % 4][:, :], ACT.Gelu, scale=scales[:, o:o + 1]).then_inc(gelu_done, 1)
                    act.wait_ge(gelu_done, HC * g + o + 5)
                    nc.scalar.activation(bh[:, o, :], hf[o % 2][:, :], ACT.Copy).then_inc(bh_done, 1)
                if first:
                    piece_hi(nc, act, pieces, stage, HC + 1, w_in, w_hi_done)
                if not last:
                    split(g + 1)

            split(0, first=True)
            piece_hi(nc, act, pieces, stage, 0, w_in, w_hi_done)
            body(0, False, first=True)
            with act.Fori(1, LAST) as g:
                body(g, False)
            body(LAST, True)

        @block.vector
        def _(dve):
            dve.sem_inc(bl_done, 2)
            dve.sem_inc(y_done, NT)
            dve.wait_ge(s_in, 32)

            def split(g):
                for c in range(0, HC, 2):
                    dve.wait_ge(ah_done, HC // 2 * g + c // 2 + 1)
                    nc.vector.tensor_tensor(al[:, c:c + 2, :], hin[:, c:c + 2, :], ah[:, c:c + 2, :].bitcast(F32), ALU.subtract).then_inc(al_done, 1)

            def body(g, last_block, first=False):
                for o in range(HC):
                    if first:
                        piece_lo(nc, dve, pieces, stage, o + 1, w_hi_done, w_lo_done)
                    dve.wait_ge(bh_done, HC * g + o + 1)
                    nc.vector.tensor_tensor(bl[:, o, :], hf[o % 2][:, :], bh[:, o, :].bitcast(F32), ALU.subtract).then_inc(bl_done, 1)
                if first:
                    piece_lo(nc, dve, pieces, stage, HC + 1, w_hi_done, w_lo_done)
                if not last_block:
                    split(g + 1)
                if first:
                    largest_low_part(nc, dve, (h2l, w3l), w_lo_done, pieces, low_max, low_done)
                for t in range(NT):
                    dve.wait_ge(y_ps, NT * g + t + 1)
                    nc.vector.tensor_tensor(y[:, t, :], ps_y[t][:, 0:D], s3[:, :], ALU.mult).then_inc(y_done, 1)
                dve.wait_ge(y_done, NT * g + 2 * NT)
                layernorm_stats(nc, dve, lambda t: y[:, t, :], st, mv, stats, STATS * g)
                dve.wait_ge(rstd, 2 * g + 2)
                if not first:
                    dve.wait_ge(out_done, 16 * g)
                for t in range(NT):
                    last = nc.vector.tensor_scalar(yo[:, t, :], y[:, t, :], mv[:, t, 0:1], rs[:, t:t + 1], ALU.subtract, ALU.mult)
                last.then_inc(n_done, 1)
                dve.wait_ge(n_done, g + 1)
                dve.wait_ge(x_in, 16 * g + 16)
                nc.vector.tensor_tensor(yo[:, :, :], yo[:, :, :], xr[:, :, :], ALU.add).then_inc(o_done, 1)

            split(0)
            piece_lo(nc, dve, pieces, stage, 0, w_hi_done, w_lo_done)
            body(0, False, first=True)
            with dve.Fori(1, LAST) as g:
                body(g, False)
            body(LAST, True)

        @block.tensor
        def _(pe):
            def body(g, exact):
                for o in range(HC):
                    pe.wait_ge(w_lo_done, o + 1)
                    pe.wait_ge(gelu_done, HC * g + o + 1)
                    dense_512(nc, ps_3[o % 4][:, :], h2h, h2l, ah, al, HC, o, exact,
                              ready=(lambda c: pe.wait_ge(al_done, HC // 2 * g + c // 2 + 1)) if o == 0 else None).then_inc(l3_ps, 1)
                pe.wait_ge(w_lo_done, len(pieces))
                pairs = passes(w3h, w3l, bh, bl, exact)
                for t in range(NT):
                    pe.wait_ge(y_done, NT * g + t + 1)
                    n = 0
                    for c in range(HC):
                        if t == 0:
                            pe.wait_ge(bl_done, HC * g + c + 3)
                        for w, a in pairs:
                            last = nc.tensor.matmul(ps_y[t][:, 0:D], a[:, c, t * P:(t + 1) * P], w[:, c, :],
                                                    start=(n == 0), stop=(n == len(pairs) * HC - 1))
                            n += 1
                    last.then_inc(y_ps, 1)

            def blocks(exact):
                with pe.Fori(1, BLOCKS) as g:
                    body(g, exact)

            body(0, False)
            by_weights(pe, low_all, low_all_done, blocks)


def build(nc, x, w_kqv, m, w1, w2, h1, h2w, w3, scales, s3, consts_in, ramp_in, out):
    env = dict(x=x, w_kqv=w_kqv, m=m, w1=w1, w2=w2, h1=h1, h2w=h2w, w3=w3, scales=scales, s3=s3, out=out,
               consts_in=consts_in, ramp_in=ramp_in)
    env["kst"] = nc.dram_tensor("kst", [B * H, 2 * HD, S], F32).ap()
    env["qst"] = nc.dram_tensor("qst", [B * H, 2 * HD + 2 * QB, S], F32).ap()
    env["vs"] = nc.dram_tensor("vs", [GROUPS, S, GH * VW], F32).ap()
    env["x1"] = nc.dram_tensor("x1", [BLOCKS, P, NT, D], F32).ap()
    env["h2"] = nc.dram_tensor("h2", [BLOCKS, P, HC, TB], F32).ap()
    with (
        nc.sbuf_tensor("consts", [P, 3 * P + 8], F32) as consts,
        nc.sbuf_tensor("ident_b", [P, P], BF16) as ident_b,
        nc.sbuf_tensor("mask_kq", [P, P], BF16) as mask_kq,
        nc.sbuf_tensor("mask_qk", [P, P], BF16) as mask_qk,
        nc.sbuf_tensor("neg_half", [P, NT], F32) as neg_half,
        nc.sbuf_tensor("eps", [P, NT], F32) as eps,
    ):
        env.update(consts=consts, ident_b=ident_b, mask_kq=mask_kq, mask_qk=mask_qk, neg_half=neg_half, eps=eps)
        with nc.sbuf_tensor("att", [P, BLOCKS * NT, D], F32) as att:
            env["att"] = att
            with ExitStack() as ctx:
                env["ramp_r"] = ctx.enter_context(nc.sbuf_tensor("ramp_r", [2 * QB + 2, S], F32R))
                for name in ("ks", "qs"):
                    env[name] = [[ctx.enter_context(nc.sbuf_tensor(f"{name}0{p}", [P, S], F32R)) for p in range(2)]]
                env["vg"] = [ctx.enter_context(nc.sbuf_tensor("vg0", [P, ST, GH * VW], F32))]
                for name in ("loaded", "ramp_set"):
                    env[name] = [ctx.enter_context(nc.semaphore(f"{name}{u}")) for u in range(2)]
                stage_projections(nc, env)
                stage_attention(nc, env)
            stage_ffn_in(nc, env)
        stage_ffn_out(nc, env)


def kernel(**inputs):
    import numpy as np
    import concourse.bacc as bacc
    from concourse import mybir as _mybir
    from concourse.bass_utils import run_bass_kernel_spmd

    get = {k.removeprefix("L0_"): np.asarray(v) for k, v in inputs.items()}
    consts = np.zeros((P, 3 * P + 8), np.float32)
    consts[:, 0:P] = np.eye(P)
    consts[:, P:2 * P] = np.tril(np.full((P, P), MASK), -1)
    consts[:, 2 * P:3 * P] = np.triu(np.full((P, P), MASK), 1)
    consts[:, 3 * P:] = np.tile(np.eye(8), (P // 8, 1))
    ramp = np.ones((2 * QB + 2, S), np.float32)
    for i in range(QB):
        ramp[i] = ramp[QB + i] = np.arange(S) - (TB * i + TB // 2)
    turned = {k: np.ascontiguousarray(get[f"ffn_{k}_w"].T) for k in ("w1", "w2", "h1", "h2", "w3")}
    scales = np.stack([get[f"ffn_{k}_s"].reshape(HC, P).T for k in ("w1", "w2", "h1", "h2")], 1)
    arrays = dict(x=get["attn_x"], w_kqv=get["attn_W_kqv"], m=get["attn_m"], w1=turned["w1"], w2=turned["w2"], h1=turned["h1"],
                  h2w=turned["h2"], w3=turned["w3"], scales=scales, s3=get["ffn_w3_s"], consts_in=consts, ramp_in=ramp)
    arrays = {f"in_{k}": np.ascontiguousarray(v) for k, v in arrays.items()}
    nc = bacc.Bacc("TRN2", target_bir_lowering=False, num_devices=1)
    args = [nc.dram_tensor(k, v.shape, _mybir.dt.from_np(v.dtype), kind="ExternalInput").ap() for k, v in arrays.items()]
    args.append(nc.dram_tensor("out_0", (B, S, D), F32, kind="ExternalOutput").ap())
    build(nc, *args)
    return run_bass_kernel_spmd(nc, [arrays], core_ids=[0]).results[0]["out_0"]
```

```python
import concourse.bass as bass
from concourse import mybir
from contextlib import ExitStack

F32 = mybir.dt.float32
F32R = mybir.dt.float32r
I32 = mybir.dt.int32
BF16 = mybir.dt.bfloat16
ALU = mybir.AluOpType
ACT = mybir.ActivationFunctionType
AX = mybir.AxisListType
RMAX = bass.bass_isa.ReduceOp.max

B, S, D = 2, 2048, 256
H = 16
HD = D // H
HID = 1024
P = 128
TB = 512
NT = TB // P
BLOCKS = B * S // TB
QB = S // TB
ST = S // P
DC = D // P
HC = HID // P
GH = 4
HG = H // GH
GROUPS = B * HG
VW = HD + 1
OW = P // GH
EPS = 1e-5
SCORE_SCALE = 1.0 / D ** 0.5

R_MIX = 3 * HD
R_CUT = R_MIX + 2 * QB
R_ALL = R_CUT + 2
HALF = 64
MASK = -1.0e30

LOADS = 4 * GH + 1
STORES = 2 * 2 * DC + 1
RAMPS = GH

W_PIECE = HID
CHECKED_PIECES = (2 * D * HID + 2 * HID * HID + HID * D) // (P * W_PIECE)
CHECK_STEPS = 6
HUGE = 2.0 ** 100


def load_ramp(eng, env, u):
    for h in range(GH):
        row = HALF * (h % 2) + R_MIX
        eng.dma_start(env["ks"][u][h // 2][row:row + 2 * QB + 2, :].bitcast(F32), env["ramp_r"][:, :].bitcast(F32)).then_inc(env["ramp_set"][u], 16)


def load_heads(eng, env, n, u, heads):
    kst, qst, loaded = env["kst"], env["qst"], env["loaded"][u]
    for h in heads:
        k, q, base = env["ks"][u][h // 2], env["qs"][u][h // 2], HALF * (h % 2)
        eng.dma_start(k[base:base + HD, :].bitcast(F32), kst[n * GH + h, 0:HD, :]).then_inc(loaded, 16)
        eng.dma_start(k[base + HD:base + R_MIX, :].bitcast(F32), kst[n * GH + h, :, :]).then_inc(loaded, 16)
        eng.dma_start(q[base:base + HD, :].bitcast(F32), qst[n * GH + h, HD:2 * HD, :]).then_inc(loaded, 16)
        eng.dma_start(q[base + HD:base + R_CUT, :].bitcast(F32), qst[n * GH + h, :, :]).then_inc(loaded, 16)


def load_values(eng, env, n, u):
    eng.dma_start(env["vg"][u][:, 0:ST * GH * VW].rearrange("p (q c) -> p q c", q=QB),
                  env["vs"][n].rearrange("q p t c -> p q (t c)")).then_inc(env["loaded"][u], 16)


STATS = 3


def layernorm_stats(nc, dve, x_of, st, mv, done, base):
    for t in range(NT):
        last = nc.vector.bn_stats(st[:, t, :], x_of(t))
    last.then_inc(done, 1)
    dve.wait_ge(done, base + 1)
    dve.sem_inc(done, 1)
    for t in range(NT):
        last = nc.vector.bn_aggr(mv[:, t, :], st[:, t, :])
    last.then_inc(done, 1)


def inverse_deviation(nc, pool, mv, tmp, rs, env, done, base):
    nc.gpsimd.tensor_tensor(tmp[:, :], mv[:, :, 1], env["eps"][:, :], ALU.add).then_inc(done, 1)
    pool.wait_ge(done, base + 1)
    nc.gpsimd.tensor_tensor(rs[:, :], tmp[:, :], env["neg_half"][:, :], ALU.pow).then_inc(done, 1)


def stage_projections(nc, env):
    consts, kst, qst, vs = env["consts"], env["kst"], env["qst"], env["vs"]
    x, w_kqv, m = env["x"], env["w_kqv"], env["m"]
    with ExitStack() as ctx:
        def sb(name, shape, dt=F32):
            return ctx.enter_context(nc.sbuf_tensor(f"qkv_{name}", shape, dt))

        def bank(name, shape=(P, TB)):
            return ctx.enter_context(nc.psum_tensor(f"qkv_{name}", list(shape), F32))

        def sem(name):
            return ctx.enter_context(nc.semaphore(f"qkv_{name}"))

        ident = consts[:, 0:P]
        sel = consts[:, 3 * P:3 * P + 8]
        w_raw = sb("w_raw", [P, DC, 3 * D])
        w_hi = sb("w_hi", [P, DC, 3 * D], F32R)
        w_lo = sb("w_lo", [P, DC, 3 * D], F32R)
        m_col = sb("m_col", [P, 1])
        m_hi = sb("m_hi", [P, 1], F32R)
        m_lo = sb("m_lo", [P, 1])
        m_a = sb("m_a", [P, QB])
        m_b = sb("m_b", [P, QB])
        m_wide = sb("m_wide", [P, QB, TB], F32R)
        xs = [env["xs"], env["xo"]]
        xn = [env["xn"], env["raw"][0]]
        st = [sb(f"st{u}", [P, NT, 6]) for u in range(2)]
        mv = [sb(f"mv{u}", [P, NT, 2]) for u in range(2)]
        tmp = [sb(f"tmp{u}", [P, NT]) for u in range(2)]
        rs = [sb(f"rs{u}", [P, NT]) for u in range(2)]
        xh = [sb(f"xh{u}", [P, DC, TB], F32R) for u in range(2)]
        xl = [sb(f"xl{u}", [P, DC, TB], F32R) for u in range(2)]
        kqh = [sb(f"kqh{u}", [P, 2 * DC, TB], F32R) for u in range(2)]
        kql = [sb(f"kql{u}", [P, 2 * DC, TB], F32R) for u in range(2)]
        vt = [sb(f"vt{u}", [P, HG, NT, GH, VW]) for u in range(2)]
        ps_x = [bank(f"ps_x{c}") for c in range(DC)]
        ps_kq = [bank(f"ps_kq{c}") for c in range(2 * DC)]
        ps_v = [bank(f"ps_v{c}", (P, 2, D)) for c in range(2)]

        ramp = sb("ramp", [2 * QB + 2, S])
        w_in = sem("w_in")
        ramp_in = sem("ramp_in")
        ramp_done = sem("ramp_done")
        x_in = [sem(f"x_in{u}") for u in range(2)]
        w_hi_done = sem("w_hi_done")
        w_lo_done = sem("w_lo_done")
        m_done = sem("m_done")
        m_out = sem("m_out")
        stats = sem("stats")
        rstd = sem("rstd")
        xn_done = sem("xn_done")
        x_t = sem("x_t")
        xh_done = sem("xh_done")
        xl_done = sem("xl_done")
        kq_ps = sem("kq_ps")
        kqh_done = sem("kqh_done")
        kql_done = sem("kql_done")
        v_ps = sem("v_ps")
        v_done = sem("v_done")
        v_ones = sem("v_ones")
        out_free = sem("out_free")
        half_done = sem("half_done")
        block = ctx.enter_context(nc.Block())
        x_blocks = x.rearrange("b (i t p) d -> (b i) p t d", p=P, t=NT)
        stored = env["stored"]

        @block.sync
        def _(sp):
            sp.dma_start(consts[:, :], env["consts_in"]).then_inc(w_in, 16)
            sp.dma_start(w_raw[:, :, :], w_kqv.rearrange("(c p) n -> p c n", p=P)).then_inc(w_in, 16)
            sp.dma_start(m_col[:, :], m.rearrange("h a b -> h (a b)").unsqueeze(1).broadcast_to([H, 8, 1])).then_inc(w_in, 16)
            sp.dma_start(ramp[:, :], env["ramp_in"]).then_inc(ramp_in, 16)
            sp.sem_inc(out_free, 2)
            sp.wait_ge(ramp_done, 1)
            load_ramp(sp, env, 0)
            sp.wait_ge(m_done, 5)
            for b in range(B):
                sp.dma_start(qst[b * H:(b + 1) * H, 2 * HD:, :],
                             m_wide[:, :, :].rearrange("p i q -> p (i q)").bitcast(F32)).then_inc(m_out, 16)

            def store_blocks(b, ii, last=False):
                for u in range(2):
                    g = QB * b + 2 * ii + u
                    sp.wait_ge(kql_done, 2 * DC * g + 4 * DC)
                    cols = bass.ds(ii * 2 * TB + u * TB, TB)
                    for c in range(DC):
                        heads = slice(b * H + c * (P // HD), b * H + (c + 1) * (P // HD))
                        for stack, src in ((kst, (kqh, kql)), (qst, (kql, kqh))):
                            chunk = c if stack is kst else DC + c
                            for k, part in enumerate(src):
                                sp.dma_start(stack[heads, k * HD:(k + 1) * HD, cols],
                                             part[u][:, chunk, :].bitcast(F32)).then_inc(stored[u], 16)
                    sp.wait_ge(v_done, 2 * g + 4)
                    dst = vs[b * HG:(b + 1) * HG, bass.ds(ii * 2 + u, 1)].rearrange("h q p t c -> p (q h) (t c)")
                    sp.dma_start(dst, vt[u][:, :, :, :, :].rearrange("p h t g c -> p h (t g c)")).then_inc(stored[u], 16)
                    if not last:
                        sp.wait_ge(stored[u], 16 * STORES * (b * QB // 2 + ii + 1))
                        sp.sem_inc(out_free, 1)

            with sp.Fori(0, QB // 2) as ii:
                store_blocks(0, ii)
            sp.wait_ge(m_out, 16 * B)
            load_heads(sp, env, 0, 0, range(GH // 2))
            with sp.Fori(0, QB // 2 - 1) as ii:
                store_blocks(1, ii)
            load_heads(sp, env, 0, 0, range(GH // 2, GH))
            load_values(sp, env, 0, 0)
            store_blocks(1, QB // 2 - 1, last=True)

        @block.gpsimd
        def _(pool):
            nc.gpsimd.memset(env["eps"][:, :], EPS)
            nc.gpsimd.memset(env["neg_half"][:, :], -0.5).then_inc(half_done, 1)
            for u in range(2):
                pool.dma_start(xs[u][:, :, :], x_blocks[u]).then_inc(x_in[u], 16)
            pool.wait_ge(half_done, 1)

            def one(g, u, load):
                pool.wait_ge(stats, STATS * g + STATS)
                inverse_deviation(nc, pool, mv[u], tmp[u], rs[u], env, rstd, 2 * g)
                if load:
                    pool.wait_ge(xn_done, g + 1)
                    pool.dma_start(xs[u][:, :, :], x_blocks[g + 2]).then_inc(x_in[u], 16)

            with pool.Fori(0, BLOCKS // 2 - 1) as r:
                for u in range(2):
                    one(2 * r + u, u, True)
            for u in range(2):
                one(BLOCKS - 2 + u, u, False)

        @block.vector
        def _(dve):
            for u in range(2):
                last = nc.vector.memset(vt[u][:, :, :, :, :], 0.0)
            last.then_inc(v_ones, 1)
            dve.wait_ge(v_ones, 1)
            for u in range(2):
                last = nc.vector.memset(vt[u][:, :, :, :, HD:HD + 1], 1.0)
            last.then_inc(v_ones, 1)
            dve.sem_inc(xl_done, DC)
            dve.sem_inc(kql_done, 2 * DC)
            def find_stats(g, u):
                dve.wait_ge(x_in[u], 8 * (g - u) + 16)
                layernorm_stats(nc, dve, lambda t: xs[u][:, t, :], st[u], mv[u], stats, STATS * g)

            def normalise(g, u):
                dve.wait_ge(rstd, 2 * g + 2)
                for t in range(NT):
                    last = nc.vector.tensor_scalar(xn[u][:, t, :], xs[u][:, t, :], mv[u][:, t, 0:1], rs[u][:, t:t + 1],
                                                   ALU.subtract, ALU.mult)
                last.then_inc(xn_done, 1)

            def x_lo(g, u):
                for c in range(DC):
                    dve.wait_ge(xh_done, DC * g + c + 1)
                    nc.vector.tensor_tensor(xl[u][:, c, :], ps_x[c][:, :], xh[u][:, c, :].bitcast(F32), ALU.subtract).then_inc(xl_done, 1)

            def kq_lo(g, u, c):
                dve.wait_ge(kqh_done, 2 * DC * g + c + 1)
                nc.vector.scalar_tensor_tensor(kql[u][:, c, :], ps_kq[c][:, :], 1.0 if c < DC else SCORE_SCALE,
                                               kqh[u][:, c, :].bitcast(F32), ALU.mult, ALU.subtract).then_inc(kql_done, 1)

            def body(g, u, more):
                if more:
                    find_stats(g + 1, 1 - u)
                dve.wait_ge(out_free, g + 1)
                kq_lo(g, u, 0)
                if more:
                    normalise(g + 1, 1 - u)
                for c in range(1, 2 * DC):
                    kq_lo(g, u, c)
                if more:
                    x_lo(g + 1, 1 - u)

            find_stats(0, 0)
            dve.wait_ge(w_in, 48)
            dve.wait_ge(w_hi_done, 1)
            nc.vector.tensor_tensor(w_lo[:, :, :], w_raw[:, :, :], w_hi[:, :, :].bitcast(F32), ALU.subtract).then_inc(w_lo_done, 1)
            normalise(0, 0)
            nc.vector.tensor_copy(env["ident_b"][:, :], ident)
            nc.vector.tensor_copy(env["mask_kq"][:, :], consts[:, P:2 * P])
            nc.vector.tensor_copy(env["mask_qk"][:, :], consts[:, 2 * P:3 * P])
            x_lo(0, 0)
            dve.wait_ge(ramp_in, 16)
            nc.vector.tensor_copy(env["ramp_r"][:, :], ramp[:, :]).then_inc(ramp_done, 1)
            nc.vector.tensor_copy(m_hi[:, :], m_col[:, :]).then_inc(m_done, 1)
            dve.wait_ge(m_done, 1)
            nc.vector.tensor_tensor(m_lo[:, :], m_col[:, :], m_hi[:, :].bitcast(F32), ALU.subtract).then_inc(m_done, 1)
            dve.wait_ge(m_done, 2)
            nc.vector.tensor_scalar(m_a[:, :], sel[:, 0:QB], m_hi[:, :].bitcast(F32), None, ALU.mult).then_inc(m_done, 1)
            dve.wait_ge(m_done, 3)
            nc.vector.scalar_tensor_tensor(m_b[:, :], sel[:, QB:2 * QB], m_lo[:, :], m_a[:, :], ALU.mult, ALU.add).then_inc(m_done, 1)
            dve.wait_ge(m_done, 4)
            nc.vector.tensor_copy(m_wide[:, :, :], m_b[:, :].unsqueeze(2).broadcast_to([P, QB, TB])).then_inc(m_done, 1)
            with dve.Fori(0, BLOCKS // 2 - 1) as r:
                for u in range(2):
                    body(2 * r + u, u, True)
            body(BLOCKS - 2, 0, True)
            body(BLOCKS - 1, 1, False)

        @block.scalar
        def _(act):
            act.wait_ge(w_in, 48)
            nc.scalar.activation(w_hi[:, :, :], w_raw[:, :, :], ACT.Copy).then_inc(w_hi_done, 1)
            act.wait_ge(v_ones, 2)
            act.sem_inc(v_done, 2)

            def x_hi(g, u):
                for c in range(DC):
                    act.wait_ge(x_t, DC * g + c + 1)
                    nc.scalar.activation(xh[u][:, c, :], ps_x[c][:, :], ACT.Copy).then_inc(xh_done, 1)

            def body(g, u, more):
                act.wait_ge(out_free, g + 1)
                for c in range(2 * DC):
                    act.wait_ge(kq_ps, 2 * DC * g + c + 1)
                    nc.scalar.activation(kqh[u][:, c, :], ps_kq[c][:, :], ACT.Copy,
                                         scale=1.0 if c < DC else SCORE_SCALE).then_inc(kqh_done, 1)
                if more:
                    x_hi(g + 1, 1 - u)
                for v in range(2):
                    act.wait_ge(v_ps, 2 * g + v + 1)
                    for t in range(2):
                        last = nc.scalar.activation(vt[u][:, :, 2 * v + t, :, 0:HD],
                                                    ps_v[v][:, t, :].rearrange("p (h g d) -> p h g d", g=GH, d=HD), ACT.Copy)
                    last.then_inc(v_done, 1)

            x_hi(0, 0)
            with act.Fori(0, BLOCKS // 2 - 1) as r:
                for u in range(2):
                    body(2 * r + u, u, True)
            body(BLOCKS - 2, 0, True)
            body(BLOCKS - 1, 1, False)

        @block.tensor
        def _(pe):
            def turn(g, u):
                pe.wait_ge(xn_done, g + 1)
                for c in range(DC):
                    pe.wait_ge(xl_done, DC * g + c + 1)
                    for t in range(NT):
                        last = nc.tensor.transpose(ps_x[c][:, t * P:(t + 1) * P], xn[u][:, t, c * P:(c + 1) * P], ident)
                    last.then_inc(x_t, 1)

            def body(g, u, more):
                pe.wait_ge(xl_done, DC * g + 2 * DC)
                for c in range(2 * DC):
                    pe.wait_ge(kql_done, 2 * DC * g + c + 1)
                    n = 0
                    for k in range(DC):
                        for w, xx in ((w_hi, xh), (w_hi, xl), (w_lo, xh)):
                            last = nc.tensor.matmul(ps_kq[c][:, :], w[:, k, c * P:(c + 1) * P], xx[u][:, k, :],
                                                    start=(n == 0), stop=(n == 3 * DC - 1))
                            n += 1
                    last.then_inc(kq_ps, 1)
                if more:
                    turn(g + 1, 1 - u)
                for v in range(2):
                    pe.wait_ge(v_done, 2 * g + v + 1)
                    for j in range(2):
                        n = 0
                        for k in range(DC):
                            for w, xx in ((w_hi, xh), (w_hi, xl), (w_lo, xh)):
                                last = nc.tensor.matmul(ps_v[v][:, j, :], xx[u][:, k, (2 * v + j) * P:(2 * v + j + 1) * P],
                                                        w[:, k, 2 * D:3 * D], start=(n == 0), stop=(n == 3 * DC - 1))
                                n += 1
                    last.then_inc(v_ps, 1)

            turn(0, 0)
            pe.wait_ge(w_lo_done, 1)
            with pe.Fori(0, BLOCKS // 2 - 1) as r:
                for u in range(2):
                    body(2 * r + u, u, True)
            body(BLOCKS - 2, 0, True)
            body(BLOCKS - 1, 1, False)


def last_stores_landed(eng, env):
    for u in range(2):
        eng.wait_ge(env["stored"][u], 16 * STORES * (BLOCKS // 2))


MAX_UNITS = [(t, p, c, e) for t in range(ST) for p in range(GH // 2) for c in range(t // NT + 1) for e in range(2)]
STEPS = [(i, j) for i in range(QB) for j in range(NT * (i + 1))]
PER_STEP = len(MAX_UNITS) // len(STEPS)
LEAD = 96
LEAD_FIRST = 64
RING = 3
P_SLOTS = 4
CUTS = 2 * GH


def first_step(i):
    return NT * i * (i + 1) // 2


def max_events(first, last):
    ends = [sum(GH * NT * (i + 1) for i in range(b + 1)) for b in range(QB)]
    out = []
    for at in range(first, last, PER_STEP):
        events = []
        for k in range(at, at + PER_STEP):
            events.append(("max", MAX_UNITS[k]))
            if k + 1 in ends:
                events.append(("finish", ends.index(k + 1)))
        if at in ends:
            events.append(("cut", ends.index(at)))
        out.append(events)
    return out


def prologue_schedule():
    return [(what, arg, 0) for events in max_events(0, LEAD_FIRST) for what, arg in events]


def spread(events):
    total, units, out = sum(what == "max" for what, _, _ in events), 0, [[] for _ in STEPS]
    for event in events:
        out[min(len(STEPS) - 1, units * len(STEPS) // total)].append(event)
        units += event[0] == "max"
    return out


def group_schedule(first=False, more=True):
    own, ahead = max_events(LEAD_FIRST if first else LEAD, len(MAX_UNITS)), max_events(0, LEAD)
    own = [[(what, arg, 0) for what, arg in events] for events in own]
    ahead = [[(what, arg, 1) for what, arg in events] for events in ahead]
    ahead[0].insert(0, ("cut", QB - 1, 0))
    if first:
        shares = spread([event for events in own + ahead for event in events])
    else:
        shares = own + (ahead if more else [ahead[0][:1]] + [[]] * (len(ahead) - 1))
    out = []
    for s, (i, j) in enumerate(STEPS):
        out.append(("scores", s, 0))
        half = len(shares[s]) // 2
        out += shares[s][:half]
        if s:
            if s - 1 == first_step(STEPS[s - 1][0]) and s > 1:
                out.append(("turn", STEPS[s - 1][0] - 1, 0))
            out.append(("values", s - 1, 0))
        out += shares[s][half:]
        if s == 2 and more:
            out.append(("load", None, 1))
        if s == len(own) + 2 and not more:
            out.append(("prepare", 0, 0))
    return out + [("values", len(STEPS) - 1, 0), ("turn", QB - 1, 0)]


RING_EVENTS = ("max", "cut", "turn")


def ring_events(schedule):
    return [x for x in schedule if x[0] in RING_EVENTS]


UNITS_PROLOGUE = len(ring_events(prologue_schedule()))
UNITS_FIRST = len(ring_events(group_schedule(first=True)))
UNITS_GROUP = len(ring_events(group_schedule()))
RING_START = RING + (-UNITS_PROLOGUE - UNITS_FIRST) % RING
assert UNITS_GROUP % RING == 0 and PER_STEP * len(STEPS) == len(MAX_UNITS)


def q_of(n):
    return RING_START + UNITS_PROLOGUE + UNITS_FIRST - UNITS_GROUP + UNITS_GROUP * n


def all_groups(eng, run):
    run(prologue_schedule(), RING_START, RING_START % RING, 0, 0)
    start = RING_START + UNITS_PROLOGUE
    run(group_schedule(first=True), start, start % RING, 0, 0)
    with eng.Fori(0, GROUPS // 2 - 1) as r:
        for u in range(2):
            run(group_schedule(), q_of(2 * r + u + 1), 0, 2 * r + u + 1, 1 - u)
    run(group_schedule(more=False), q_of(GROUPS - 1), 0, GROUPS - 1, 1)


def stage_attention(nc, env):
    att, loaded, ramp_set = env["att"], env["loaded"], env["ramp_set"]
    with ExitStack() as ctx:
        def sb(name, shape, dt=F32):
            return ctx.enter_context(nc.sbuf_tensor(f"att_{name}", shape, dt))

        def bank(name, shape=(P, TB)):
            return ctx.enter_context(nc.psum_tensor(f"att_{name}", list(shape), F32))

        def sem(name):
            return ctx.enter_context(nc.semaphore(f"att_{name}"))

        ident = env["consts"][:, 0:P]
        part_max = sb("part_max", [P, GH, ST, QB])
        neg_max = [sb(f"neg_max{n}", [P, P // NT, NT]) for n in range(2)]
        cut_hi = [sb(f"cut_hi{n}", [GH * NT, P], F32R) for n in range(2)]
        cut_lo = [sb(f"cut_lo{n}", [GH * NT, P], F32R) for n in range(2)]
        inv = sb("inv", [P, NT * GH])
        for name in ("ks", "qs"):
            env[name].append([sb(f"{name}1{p}", [P, S], F32R) for p in range(2)])
        env["vg"].append(sb("vg1", [P, ST * GH * VW + OW - VW]))
        ks, qs, vg = env["ks"], env["qs"], env["vg"]
        o_t = sb("o_t", [P, TB])
        probs = [sb(f"probs{n}", [P, GH, TB]) for n in range(P_SLOTS)]
        ps_s = [bank(f"ps_s{p}", (P, 2, TB)) for p in range(2)]
        ring = [bank(f"ring{n}") for n in range(RING)]
        ps_o = bank("ps_o")

        cut_set = sem("cut_set")
        scores_ps = sem("scores_ps")
        exp_done = sem("exp_done")
        pv_done = sem("pv_done")
        o_copied = sem("o_copied")
        tail_set = sem("tail_set")
        ring_ps = sem("ring_ps")
        ring_used = sem("ring_used")
        max_done = sem("max_done")
        cut_part = sem("cut_part")
        inv_done = sem("inv_done")
        raw_in, checked, total_max_done, inexact_done = (sem(n) for n in ("raw_in", "checked", "total_max_done", "inexact_done"))
        hi_part = sb("hi_part", [P, W_PIECE], F32R)
        diff, total, total_max = sb("diff", [P, W_PIECE]), sb("total", [P, W_PIECE]), sb("total_max", [P, 1])
        sp_turns, pool_turns = sem("sp_turns"), sem("pool_turns")
        block = ctx.enter_context(nc.Block())

        @block.sync
        def _(sp):
            last_stores_landed(sp, env)
            load_ramp(sp, env, 1)
            sp.dma_start(env["scales_sb"][:, :, :], env["scales"]).then_inc(env["scales_in"], 16)
            sp.dma_start(env["s3_sb"][:, :], env["s3"].partition_broadcast(P)).then_inc(env["scales_in"], 16)
            sp.dma_start(env["xs"][:, :, :], env["x"].rearrange("b (i t p) d -> (b i) p t d", p=P, t=NT)[0]).then_inc(env["x_in"], 16)

            def cuts(schedule, q0, bank0, n, u):
                k = -1
                for what, i, ahead in schedule:
                    k += what in RING_EVENTS
                    if what == "prepare":
                        sp.wait_ge(checked, CHECK_STEPS * CHECKED_PIECES + 1)
                        for p in range(2):
                            sp.dma_start(staged(env["raw"], p, DC), first_layer_piece(env, p)).then_inc(env["w_in"][p], 16)
                    if what == "load":
                        sp.wait_ge(pv_done, len(STEPS) * n + P_SLOTS)
                        sp.sem_inc(sp_turns, 1)
                        load_heads(sp, env, n + 1, 1 - u, range(GH))
                        load_values(sp, env, n + 1, 1 - u)
                    if what != "cut":
                        continue
                    w = QB * (n + ahead) + i
                    sp.wait_ge(ring_used, q0 + k + 1)
                    sp.sem_inc(sp_turns, 1)
                    if not (isinstance(w, int) and w == 0):
                        sp.wait_ge(cut_set, 16 * CUTS * w)
                    for h in range(GH):
                        p, base = h // 2, HALF * (h % 2)
                        for r, src in enumerate((cut_hi, cut_lo)):
                            row = base + R_CUT + r
                            sp.dma_start(qs[(u + ahead) % 2][p][row:row + 1, i * TB:(i + 1) * TB].bitcast(F32),
                                         src[i % 2][h * NT:(h + 1) * NT, :].bitcast(F32)).then_inc(cut_set, 16)

            all_groups(sp, cuts)

        @block.gpsimd
        def _(pool):
            last_stores_landed(pool, env)
            find_inexact(nc, pool, env, raw_in, hi_part, diff, total, checked, pool_turns)
            pool.wait_ge(total_max_done, 1)
            nc.gpsimd.partition_all_reduce(env["inexact"][:, :], total_max[:, :], P, RMAX).then_inc(inexact_done, 1)
            pool.wait_ge(inexact_done, 1)
            with pool.Fori(0, 2) as k:
                pool.wait_ge(env["stats"], STATS * k + STATS)
                inverse_deviation(nc, pool, env["mv"], env["tmp"], env["rs"], env, env["rstd"], 2 * k)

        @block.scalar
        def _(act):
            last_stores_landed(act, env)
            act.sem_inc(exp_done, 2)
            act.sem_inc(o_copied, 1)

            def group(n):
                for s, (i, j) in enumerate(STEPS):
                    skip = max(0, (j - NT * i) * P)
                    for p in range(2):
                        act.wait_ge(scores_ps, 2 * len(STEPS) * n + 2 * s + p + 1)
                        if p == 0:
                            act.wait_ge(pv_done, len(STEPS) * n + s + 1)
                        nc.scalar.activation(probs[s % P_SLOTS][:, 2 * p:2 * p + 2, skip:TB], ps_s[p][:, :, skip:TB],
                                             ACT.Exp).then_inc(exp_done, 1)
                    if s == first_step(i) and i > 0:
                        copy_out(n, i - 1)
                copy_out(n, QB - 1)

            def copy_out(n, i):
                last_step = first_step(i + 1) - 1
                act.wait_ge(pv_done, len(STEPS) * n + last_step + 1 + P_SLOTS)
                nc.scalar.activation(o_t[:, :], ps_o[:, :], ACT.Copy).then_inc(o_copied, 1)

            with act.Fori(0, GROUPS) as n:
                group(n)

        @block.vector
        def _(dve):
            dve.sem_inc(ring_used, RING_START)
            for n in range(2):
                nc.vector.memset(neg_max[n][:, GH:, :], 0.0)
            for u in range(2):
                last = nc.vector.memset(vg[u][:, ST * GH * VW:], 0.0)
            last.then_inc(tail_set, 1)

            def run(schedule, q0, bank0, n, u):
                q = k = 0
                for what, arg, ahead in schedule:
                    if what in ("scores", "values", "load"):
                        continue
                    q, bank = q0 + k, (bank0 + k) % RING
                    if what == "prepare":
                        dve.wait_ge(checked, CHECK_STEPS * CHECKED_PIECES + 1)
                        nc.vector.reduce_max(total_max[:, :], total[:, :], axis=AX.X).then_inc(total_max_done, 1)
                        dve.wait_ge(ring_used, q)
                        prepare(nc, dve, env, arg, first=True)
                        continue
                    if what == "finish":
                        dve.wait_ge(ring_used, q)
                        nc.vector.tensor_reduce(neg_max[arg % 2][:, 0:GH, :], part_max[:, :, NT * arg:NT * (arg + 1), 0:arg + 1],
                                                op=ALU.max, axis=AX.X, negate=True).then_inc(max_done, 1)
                        continue
                    dve.wait_ge(ring_ps, q + 1)
                    if what == "max":
                        t, p, c, e = arg
                        w = P * (t % NT + 1) if c == t // NT else TB
                        nc.vector.reduce_max(part_max[:, 2 * p + e, t, c:c + 1], ring[bank][:, 0:w], axis=AX.X).then_inc(ring_used, 1)
                    elif what == "cut":
                        w = QB * (n + ahead) + arg
                        if not (isinstance(w, int) and w < 2):
                            dve.wait_ge(cut_set, 16 * CUTS * (w - 1))
                        nc.vector.tensor_copy(cut_hi[arg % 2][:, :], ring[bank][0:GH * NT, 0:P]).then_inc(cut_part, 1)
                        dve.wait_ge(cut_part, w + 1)
                        nc.vector.tensor_tensor(cut_lo[arg % 2][:, :], ring[bank][0:GH * NT, 0:P], cut_hi[arg % 2][:, :].bitcast(F32),
                                                ALU.subtract).then_inc(ring_used, 1)
                    else:
                        o = ring[bank][:, :].rearrange("p (g c) -> p g c", c=OW)
                        dve.wait_ge(ring_used, q)
                        nc.vector.reciprocal(inv[:, :], o[:, :, HD]).then_inc(inv_done, 1)
                        dve.wait_ge(inv_done, QB * n + arg + 1)
                        dst = att[:, bass.ds(n // HG * ST + NT * arg, NT), bass.ds(n % HG * (GH * HD), GH * HD)].rearrange("p t (h d) -> p t h d", d=HD)
                        nc.vector.tensor_tensor(dst, o[:, :, 0:HD].rearrange("p (t h) d -> p t h d", h=GH),
                                                inv[:, :].rearrange("p (t h) -> p t h", h=GH).unsqueeze(3).broadcast_to([P, NT, GH, HD]),
                                                ALU.mult).then_inc(ring_used, 1)
                    k += 1

            all_groups(dve, run)

        @block.tensor
        def _(pe):
            pe.sem_inc(pv_done, P_SLOTS)

            def scores(n, u, s):
                i, j = STEPS[s]
                if j == 0:
                    pe.wait_ge(cut_set, 16 * CUTS * (QB * n + i + 1))
                skip = max(0, (j - NT * i) * P)
                for p in range(2):
                    pe.wait_ge(exp_done, 2 * len(STEPS) * n + 2 * s + p + 1)
                    for e in range(2):
                        rows = slice(HALF * e, HALF * e + R_ALL)
                        last = nc.tensor.matmul(ps_s[p][:, e, skip:TB], ks[u][p][rows, j * P:(j + 1) * P],
                                                qs[u][p][rows, i * TB + skip:(i + 1) * TB], start=True, stop=j < NT * i)
                    if j >= NT * i:
                        for e in range(2):
                            last = nc.tensor.matmul(ps_s[p][:, e, skip:skip + P], env["ident_b"][:, :], env["mask_kq"][:, :],
                                                    start=False, stop=True)
                    last.then_inc(scores_ps, 1)

            def values(n, u, s):
                i, j = STEPS[s]
                skip = max(0, (j - NT * i) * P)
                pe.wait_ge(exp_done, 2 * len(STEPS) * n + 2 * s + 2 + 2)
                if j == 0:
                    pe.wait_ge(o_copied, QB * n + i + 1)
                for h in range(GH):
                    col = (GH * j + h) * VW
                    last = nc.tensor.matmul(ps_o[OW * h:OW * (h + 1), skip:TB], vg[u][:, col:col + OW],
                                            probs[s % P_SLOTS][:, h, skip:TB], start=(j == 0), stop=(j == NT * (i + 1) - 1))
                last.then_inc(pv_done, 1)

            def run(schedule, q0, bank0, n, u):
                k = 0
                for what, arg, ahead in schedule:
                    if what == "scores":
                        scores(n, u, arg)
                    elif what == "values":
                        values(n, u, arg)
                    elif what in RING_EVENTS:
                        pe.wait_ge(ring_used, q0 + k - RING + 1)
                        if what == "max":
                            if arg == MAX_UNITS[0] and ahead:
                                pe.wait_ge(ramp_set[1 - u], 16 * RAMPS)
                                pe.wait_ge(loaded[1 - u], load_count(n + 1, 1 - u))
                            last = max_unit(ring[(bank0 + k) % RING], arg, (u + ahead) % 2)
                        elif what == "cut":
                            pe.wait_ge(max_done, QB * (n + ahead) + arg + 1)
                            last = nc.tensor.transpose(ring[(bank0 + k) % RING][:, 0:P], neg_max[arg % 2][:, :, :].rearrange("p h t -> p (h t)"), ident)
                        else:
                            pe.wait_ge(o_copied, QB * n + arg + 2)
                            for t in range(NT):
                                last = nc.tensor.transpose(ring[(bank0 + k) % RING][:, t * P:(t + 1) * P], o_t[:, t * P:(t + 1) * P], ident)
                        last.then_inc(ring_ps, 1)
                        k += 1

            def max_unit(bank, arg, u):
                t, p, c, e = arg
                diagonal = c == t // NT
                w = P * (t % NT + 1) if diagonal else TB
                rows = slice(HALF * e, HALF * e + R_CUT)
                last = nc.tensor.matmul(bank[:, 0:w], qs[u][p][rows, t * P:(t + 1) * P],
                                        ks[u][p][rows, c * TB:c * TB + w], start=True, stop=not diagonal)
                if diagonal:
                    last = nc.tensor.matmul(bank[:, w - P:w], env["ident_b"][:, :], env["mask_qk"][:, :], start=False, stop=True)
                return last

            def load_count(n, u):
                return 8 * LOADS * (n - u) + 16 * LOADS

            pe.sem_inc(ring_ps, RING_START)
            pe.wait_ge(tail_set, 1)
            pe.wait_ge(ramp_set[0], 16 * RAMPS)
            pe.wait_ge(loaded[0], 16 * LOADS)
            all_groups(pe, run)




def weight_piece(src, hi, lo, o, n):
    chunks = src.shape[0] // P
    assert chunks * n == W_PIECE
    return src.rearrange("(c p) n -> p c n", p=P)[:, :, o:o + n], hi[:, :, o:o + n], lo[:, :, o:o + n], chunks


def staged(stage, n, chunks):
    return stage[n % 2][:, :, :].rearrange("p t d -> p (t d)").rearrange("p (c n) -> p c n", c=chunks)


def load_pieces(sp, pieces, stage, w_in, w_lo_done, there=0):
    for n, (src, _, _, chunks) in enumerate(pieces):
        if n < there:
            continue
        if n >= 2:
            sp.wait_ge(w_lo_done, n - 1)
        sp.dma_start(staged(stage, n, chunks), src).then_inc(w_in[n % 2], 16)


def piece_hi(nc, act, pieces, stage, n, w_in, w_hi_done):
    _, hi, _, chunks = pieces[n]
    act.wait_ge(w_in[n % 2], 16 * (n // 2 + 1))
    nc.scalar.activation(hi, staged(stage, n, chunks), ACT.Copy).then_inc(w_hi_done, 1)


def piece_lo(nc, dve, pieces, stage, n, w_hi_done, w_lo_done):
    _, hi, lo, chunks = pieces[n]
    dve.wait_ge(w_hi_done, n + 1)
    nc.vector.tensor_tensor(lo, staged(stage, n, chunks), hi.bitcast(F32), ALU.subtract).then_inc(w_lo_done, 1)


def find_inexact(nc, pool, env, raw_in, hi, diff, total, done, turns):
    raw = [r[:, :, :].rearrange("p t d -> p (t d)") for r in env["raw"]]
    nc.gpsimd.memset(total[:, :], 0.0).then_inc(done, 1)
    base = 0
    for name in ("w1", "w2", "h1", "h2w", "w3"):
        flat = env[name].rearrange("(p a) n -> p (a n)", p=P)
        with pool.Fori(0, flat.shape[1] // (2 * W_PIECE)) as r:
            for u in range(2):
                n = base + 2 * r + u
                pool.wait_ge(done, CHECK_STEPS * n + 1)
                pool.dma_start(raw[u], flat[:, bass.ds(r * 2 * W_PIECE + u * W_PIECE, W_PIECE)]).then_inc(raw_in, 16)
                pool.wait_ge(raw_in, 16 * n + 16)
                pool.sem_inc(turns, 1)
                nc.gpsimd.tensor_copy(hi[:, :], raw[u]).then_inc(done, 1)
                pool.wait_ge(done, CHECK_STEPS * n + 2)
                pool.sem_inc(turns, 1)
                nc.gpsimd.tensor_tensor(diff[:, :], raw[u], hi[:, :].bitcast(F32), ALU.subtract).then_inc(done, 1)
                pool.wait_ge(done, CHECK_STEPS * n + 3)
                pool.sem_inc(turns, 1)
                nc.gpsimd.tensor_scalar(diff[:, :], diff[:, :], HUGE, 1.0, ALU.mult, ALU.min).then_inc(done, 1)
                pool.wait_ge(done, CHECK_STEPS * n + 4)
                pool.sem_inc(turns, 1)
                nc.gpsimd.tensor_scalar(diff[:, :], diff[:, :], -1.0, None, ALU.max).then_inc(done, 1)
                pool.wait_ge(done, CHECK_STEPS * n + 5)
                pool.sem_inc(turns, 1)
                nc.gpsimd.tensor_tensor(diff[:, :], diff[:, :], diff[:, :], ALU.mult).then_inc(done, 1)
                pool.wait_ge(done, CHECK_STEPS * n + 6)
                pool.sem_inc(turns, 1)
                nc.gpsimd.tensor_tensor(total[:, :], total[:, :], diff[:, :], ALU.add).then_inc(done, 1)
        base += flat.shape[1] // W_PIECE


def by_weights(pe, env, blocks):
    bits = pe.value_load(env["inexact"][0:1, 0:1].bitcast(I32), min_val=0, max_val=2 ** 31 - 1)
    with pe.If(bits == 0):
        blocks(True)
    with pe.Else():
        blocks(False)


def passes(w_hi, w_lo, x_hi, x_lo, exact):
    return ((w_hi, x_hi), (w_hi, x_lo)) if exact else ((w_hi, x_hi), (w_hi, x_lo), (w_lo, x_hi))


def dense_512(nc, out, w_hi, w_lo, x_hi, x_lo, chunks, o, exact, ready=None):
    pairs = passes(w_hi, w_lo, x_hi, x_lo, exact)
    n = 0
    for c in range(chunks):
        if ready:
            ready(c)
        for w, xx in pairs:
            last = nc.tensor.matmul(out, w[:, c, o * P:(o + 1) * P], xx[:, c, :], start=(n == 0), stop=(n == len(pairs) * chunks - 1))
            n += 1
    return last


def prepare(nc, dve, env, g, first=False):
    st, mv, rs, xs, xo, xn = (env[n] for n in ("st", "mv", "rs", "xs", "xo", "xn"))
    stats, rstd, a_done, x1_done = (env[n] for n in ("stats", "rstd", "a_done", "x1_done"))
    a = env["att"][:, bass.ds(g * NT, NT), :]
    dve.wait_ge(env["x_in"], 16 * g + 16)
    layernorm_stats(nc, dve, lambda t: a[:, t, :], st, mv, stats, 2 * STATS * g)
    dve.wait_ge(rstd, 4 * g + 2)
    for t in range(NT):
        last = nc.vector.tensor_scalar(xn[:, t, :], a[:, t, :], mv[:, t, 0:1], rs[:, t:t + 1], ALU.subtract, ALU.mult)
    last.then_inc(a_done, 1)
    dve.wait_ge(a_done, g + 1)
    if not first:
        dve.wait_ge(env["x1_out"], 16 * g)
    nc.vector.tensor_tensor(xo[:, :, :], xn[:, :, :], xs[:, :, :], ALU.add).then_inc(x1_done, 1)
    dve.wait_ge(x1_done, g + 1)
    layernorm_stats(nc, dve, lambda t: xo[:, t, :], st, mv, stats, 2 * STATS * g + STATS)
    dve.wait_ge(rstd, 4 * g + 4)
    for t in range(NT):
        last = nc.vector.tensor_scalar(xn[:, t, :], xo[:, t, :], mv[:, t, 0:1], rs[:, t:t + 1], ALU.subtract, ALU.mult)
    last.then_inc(env["xn_done"], 1)


def first_layer_piece(env, n):
    src, wide = env[("w1", "w2")[n % 2]], W_PIECE // DC
    return src.rearrange("(c p) n -> p c n", p=P)[:, :, n // 2 * wide:(n // 2 + 1) * wide]


def second_half_piece(env, n):
    return env["h2w"].rearrange("(c p) n -> p c n", p=P)[:, :, n * P:(n + 1) * P]


def stage_ffn_in(nc, env):
    x, att, x1, h2 = env["x"], env["att"], env["x1"], env["h2"]
    with ExitStack() as ctx:
        def sb(name, shape, dt=F32):
            return ctx.enter_context(nc.sbuf_tensor(f"fin_{name}", shape, dt))

        def bank(name, shape=(P, TB)):
            return ctx.enter_context(nc.psum_tensor(f"fin_{name}", list(shape), F32))

        def sem(name):
            return ctx.enter_context(nc.semaphore(f"fin_{name}"))

        ident = env["consts"][:, 0:P]
        w1h, w1l, w2h, w2l = (sb(n, [P, DC, HID], F32R) for n in ("w1h", "w1l", "w2h", "w2l"))
        h1h, h1l = (sb(n, [P, HC, HID], F32R) for n in ("h1h", "h1l"))
        scales = env["scales_sb"]
        xs, xo, xn = env["xs"], env["xo"], env["xn"]
        mv, tmp, rs = env["mv"], env["tmp"], env["rs"]
        xh, xl = sb("xh", [P, DC, TB], F32R), sb("xl", [P, DC, TB], F32R)
        gate = [sb(f"gate{n}", [P, TB]) for n in range(2)]
        hf = [sb(f"hf{n}", [P, TB]) for n in range(2)]
        hh, hl = sb("hh", [P, HC, TB], F32R), sb("hl", [P, HC, TB], F32R)
        HALFC = HC // 2
        ho = sb("ho", [P, HALFC, TB])
        ps_x = [bank(f"ps_x{c}") for c in range(DC)]
        ps_1 = [bank(f"ps_1{n}", (P, 2, TB)) for n in range(2)]
        ps_2 = [bank(f"ps_2{n}") for n in range(2)]

        w_in = env["w_in"]
        x_in, stats, rstd, x1_done, xn_done, x1_out = (env[n] for n in ("x_in", "stats", "rstd", "x1_done", "xn_done", "x1_out"))
        names = ("w_hi_done w_lo_done x_t xh_done xl_done l1_ps gate_done "
                 "hf_done hh_done hl_done l2_ps gelu_done h2_out h2_free")
        (w_hi_done, w_lo_done, x_t, xh_done, xl_done, l1_ps, gate_done,
         hf_done, hh_done, hl_done, l2_ps, gelu_done, h2_out, h2_free) = (sem(n) for n in names.split())
        stage = env["raw"]
        WIDE = W_PIECE // DC
        pieces = []
        for o in range(0, HID, WIDE):
            pieces += [weight_piece(env["w1"], w1h, w1l, o, WIDE), weight_piece(env["w2"], w2h, w2l, o, WIDE)]
        LAYER1_PIECES = len(pieces)
        pieces += [weight_piece(env["h1"], h1h, h1l, o * P, P) for o in range(HC)]
        block = ctx.enter_context(nc.Block())
        x_blocks = x.rearrange("b (i t p) d -> (b i) p t d", p=P, t=NT)
        LAST = BLOCKS - 1

        @block.sync
        def _(sp):
            sp.dma_start(x1[0], xo[:, :, :]).then_inc(x1_out, 16)
            sp.dma_start(xs[:, :, :], x_blocks[1]).then_inc(x_in, 16)
            load_pieces(sp, pieces, stage, w_in, w_lo_done, there=2)
            sp.sem_inc(h2_free, 1)

            def body(g, last):
                if not last:
                    sp.wait_ge(x1_done, g + 2)
                    sp.dma_start(x1[g + 1], xo[:, :, :]).then_inc(x1_out, 16)
                for k in range(2):
                    sp.wait_ge(gelu_done, HC * g + HALFC * (k + 1) + 2)
                    sp.dma_start(h2[g, :, HALFC * k:HALFC * (k + 1), :], ho[:, :, :]).then_inc(h2_out, 16)
                    sp.wait_ge(h2_out, 32 * g + 16 * (k + 1))
                    sp.sem_inc(h2_free, 1)

            with sp.Fori(0, LAST - 1) as g:
                sp.wait_ge(x1_done, g + 2)
                sp.dma_start(xs[:, :, :], x_blocks[g + 2]).then_inc(x_in, 16)
                body(g, False)
            body(LAST - 1, False)
            sp.wait_ge(w_lo_done, len(pieces))
            for n in range(2):
                sp.dma_start(staged(stage, n, HC), second_half_piece(env, n)).then_inc(env["w2_in"][n], 16)
            sp.dma_start(env["hin"], h2[0]).then_inc(env["h_first"], 16)
            body(LAST, True)
            sp.wait_ge(x1_out, 16 * BLOCKS)

        @block.gpsimd
        def _(pool):
            def deviations(first, last):
                with pool.Fori(first, last) as k:
                    pool.wait_ge(stats, STATS * k + STATS)
                    inverse_deviation(nc, pool, mv, tmp, rs, env, rstd, 2 * k)

            deviations(2, 2 * BLOCKS)

        @block.scalar
        def _(act):
            act.wait_ge(env["scales_in"], 32)
            act.sem_inc(gelu_done, 2)

            def x_parts(g):
                for c in range(DC):
                    act.wait_ge(x_t, DC * g + c + 1)
                    nc.scalar.activation(xh[:, c, :], ps_x[c][:, :], ACT.Copy).then_inc(xh_done, 1)

            def hidden_hi(g, o):
                act.wait_ge(hf_done, HC * g + o + 3)
                nc.scalar.activation(hh[:, o, :], hf[o % 2][:, :], ACT.Copy).then_inc(hh_done, 1)

            def body(g, last, first=False):
                for o in range(HC):
                    act.wait_ge(l1_ps, HC * g + o + 1)
                    nc.scalar.activation(gate[o % 2][:, :], ps_1[o % 2][:, 0, :], ACT.Silu, scale=scales[:, 0, o:o + 1]).then_inc(gate_done, 1)
                    if o:
                        hidden_hi(g, o - 1)
                    if first:
                        piece_hi(nc, act, pieces, stage, LAYER1_PIECES + o, w_in, w_hi_done)
                hidden_hi(g, HC - 1)
                for o in range(HC):
                    if o % HALFC == 0:
                        act.wait_ge(h2_free, 2 * g + o // HALFC + 1)
                    act.wait_ge(l2_ps, HC * g + o + 1)
                    nc.scalar.activation(ho[:, o % HALFC, :], ps_2[o % 2][:, :], ACT.Gelu, scale=scales[:, 2, o:o + 1]).then_inc(gelu_done, 1)
                    if o == HALFC - 1 and not last:
                        x_parts(g + 1)

            for n in range(2):
                piece_hi(nc, act, pieces, stage, n, w_in, w_hi_done)
            x_parts(0)
            for n in range(2, LAYER1_PIECES):
                piece_hi(nc, act, pieces, stage, n, w_in, w_hi_done)
            body(0, False, first=True)
            with act.Fori(1, LAST) as g:
                body(g, False)
            body(LAST, True)

        @block.vector
        def _(dve):
            dve.sem_inc(hf_done, 2)
            dve.sem_inc(hl_done, 2)

            def x_parts(g):
                for c in range(DC):
                    dve.wait_ge(xh_done, DC * g + c + 1)
                    nc.vector.tensor_tensor(xl[:, c, :], ps_x[c][:, :], xh[:, c, :].bitcast(F32), ALU.subtract).then_inc(xl_done, 1)

            def hidden_lo(g, o):
                dve.wait_ge(hh_done, HC * g + o + 1)
                nc.vector.tensor_tensor(hl[:, o, :], hf[o % 2][:, :], hh[:, o, :].bitcast(F32), ALU.subtract).then_inc(hl_done, 1)

            def layer1(g, first=False):
                for o in range(HC):
                    dve.wait_ge(gate_done, HC * g + o + 1)
                    dve.wait_ge(hl_done, HC * g + o + 1)
                    nc.vector.scalar_tensor_tensor(hf[o % 2][:, :], ps_1[o % 2][:, 1, :], scales[:, 1, o:o + 1], gate[o % 2][:, :],
                                                   ALU.mult, ALU.mult).then_inc(hf_done, 1)
                    if o:
                        hidden_lo(g, o - 1)
                    if first:
                        piece_lo(nc, dve, pieces, stage, LAYER1_PIECES + o, w_hi_done, w_lo_done)
                hidden_lo(g, HC - 1)

            for n in range(2):
                piece_lo(nc, dve, pieces, stage, n, w_hi_done, w_lo_done)
            x_parts(0)
            for n in range(2, LAYER1_PIECES):
                piece_lo(nc, dve, pieces, stage, n, w_hi_done, w_lo_done)
            layer1(0, first=True)
            prepare(nc, dve, env, 1)
            x_parts(1)
            with dve.Fori(1, LAST) as g:
                layer1(g)
                prepare(nc, dve, env, g + 1)
                x_parts(g + 1)
            layer1(LAST)

        @block.tensor
        def _(pe):
            def turn(g):
                pe.wait_ge(xn_done, g + 1)
                for c in range(DC):
                    for t in range(NT):
                        last = nc.tensor.transpose(ps_x[c][:, t * P:(t + 1) * P], xn[:, t, c * P:(c + 1) * P], ident)
                    last.then_inc(x_t, 1)

            def body(g, last_block, exact):
                pe.wait_ge(xh_done, DC * g + DC)
                pe.wait_ge(xl_done, DC * g + DC)
                for o in range(HC):
                    pe.wait_ge(w_lo_done, 2 * (o * P // WIDE) + 2)
                    pe.wait_ge(hf_done, HC * g + o + 1)
                    dense_512(nc, ps_1[o % 2][:, 0, :], w1h, w1l, xh, xl, DC, o, exact)
                    dense_512(nc, ps_1[o % 2][:, 1, :], w2h, w2l, xh, xl, DC, o, exact).then_inc(l1_ps, 1)
                for o in range(HC):
                    pe.wait_ge(w_lo_done, LAYER1_PIECES + o + 1)
                    pe.wait_ge(gelu_done, HC * g + o + 1)
                    dense_512(nc, ps_2[o % 2][:, :], h1h, h1l, hh, hl, HC, o, exact,
                              ready=(lambda c: pe.wait_ge(hl_done, HC * g + c + 3)) if o == 0 else None).then_inc(l2_ps, 1)
                    if o == HALFC - 1 and not last_block:
                        turn(g + 1)

            def blocks(exact):
                with pe.Fori(0, LAST) as g:
                    body(g, False, exact)
                body(LAST, True, exact)

            turn(0)
            by_weights(pe, env, blocks)


def stage_ffn_out(nc, env):
    x1, h2, out = env["x1"], env["h2"], env["out"]
    with ExitStack() as ctx:
        def sb(name, shape, dt=F32):
            return ctx.enter_context(nc.sbuf_tensor(f"fout_{name}", shape, dt))

        def bank(name, shape=(P, TB)):
            return ctx.enter_context(nc.psum_tensor(f"fout_{name}", list(shape), F32))

        def sem(name):
            return ctx.enter_context(nc.semaphore(f"fout_{name}"))

        h2h, h2l = (sb(n, [P, HC, HID], F32R) for n in ("h2h", "h2l"))
        w3h, w3l = (sb(n, [P, HC, D], F32R) for n in ("w3h", "w3l"))
        scales, s3 = env["scales_sb"], env["s3_sb"]
        hin = env["hin"]
        ah, al = sb("ah", [P, HC, TB], F32R), sb("al", [P, HC, TB], F32R)
        hf = [sb(f"hg{n}", [P, TB]) for n in range(2)]
        bh, bl = sb("bh", [P, HC, TB], F32R), sb("bl", [P, HC, TB], F32R)
        xr, y, yo = env["xs"], env["xn"], env["xo"]
        st, mv, tmp, rs = sb("st", [P, NT, 6]), sb("mv", [P, NT, 2]), sb("tmp", [P, NT]), sb("rs", [P, NT])
        ps_3 = [bank(f"ps_3{n}") for n in range(4)]
        ps_y = [bank(f"ps_y{n}") for n in range(4)]
        w_in = env["w2_in"]
        names = ("w_hi_done2 w_lo_done2 h_in x_in2 stats2 rstd2 ah_done al_done l3_ps gelu_done2 bh_done bl_done "
                 "y_ps y_done n_done o_done out_done")
        (w_hi_done, w_lo_done, h_in, x_in, stats, rstd, ah_done, al_done, l3_ps, gelu_done, bh_done, bl_done,
         y_ps, y_done, n_done, o_done, out_done) = (sem(n) for n in names.split())
        stage = env["raw"]
        pieces = [weight_piece(env["h2w"], h2h, h2l, o * P, P) for o in range(HC)]
        pieces += [weight_piece(env["w3"], w3h, w3l, o * P, P) for o in range(DC)]
        block = ctx.enter_context(nc.Block())
        LAST = BLOCKS - 1
        out_blocks = out.rearrange("b (i t p) d -> (b i) p t d", p=P, t=NT)

        @block.sync
        def _(sp):
            load_pieces(sp, pieces, stage, w_in, w_lo_done, there=2)
            sp.dma_start(xr[:, :, :], x1[0]).then_inc(x_in, 16)

            def body(g, last):
                if not last:
                    sp.wait_ge(al_done, HC // 2 * g + HC // 2)
                    sp.dma_start(hin, h2[g + 1]).then_inc(h_in, 16)
                sp.wait_ge(o_done, g + 1)
                if not last:
                    sp.dma_start(out_blocks[g], yo[:, :, :]).then_inc(out_done, 16)
                    sp.dma_start(xr[:, :, :], x1[g + 1]).then_inc(x_in, 16)
                else:
                    for k in range(2):
                        half = slice(k * NT // 2, (k + 1) * NT // 2)
                        sp.wait_ge(o_done, g + k + 1)
                        sp.dma_start(out_blocks[g][:, half, :], yo[:, half, :]).then_inc(out_done, 16)

            with sp.Fori(0, LAST) as g:
                body(g, False)
            body(LAST, True)
            sp.wait_ge(out_done, 16 * (BLOCKS + 1))

        @block.gpsimd
        def _(pool):
            with pool.Fori(0, BLOCKS) as k:
                pool.wait_ge(stats, STATS * k + STATS)
                inverse_deviation(nc, pool, mv, tmp, rs, env, rstd, 2 * k)

        @block.scalar
        def _(act):
            act.sem_inc(gelu_done, 4)

            def split(g, first=False):
                if first:
                    act.wait_ge(env["h_first"], 16)
                else:
                    act.wait_ge(h_in, 16 * g)
                for c in range(0, HC, 2):
                    nc.scalar.activation(ah[:, c:c + 2, :], hin[:, c:c + 2, :], ACT.Copy).then_inc(ah_done, 1)

            def body(g, last, first=False):
                for o in range(HC):
                    if first:
                        piece_hi(nc, act, pieces, stage, o + 1, w_in, w_hi_done)
                    act.wait_ge(l3_ps, HC * g + o + 1)
                    act.wait_ge(bl_done, HC * g + o + 1)
                    nc.scalar.activation(hf[o % 2][:, :], ps_3[o % 4][:, :], ACT.Gelu, scale=scales[:, 3, o:o + 1]).then_inc(gelu_done, 1)
                    act.wait_ge(gelu_done, HC * g + o + 5)
                    nc.scalar.activation(bh[:, o, :], hf[o % 2][:, :], ACT.Copy).then_inc(bh_done, 1)
                if first:
                    piece_hi(nc, act, pieces, stage, HC + 1, w_in, w_hi_done)
                if not last:
                    split(g + 1)

            piece_hi(nc, act, pieces, stage, 0, w_in, w_hi_done)
            split(0, first=True)
            body(0, False, first=True)
            with act.Fori(1, LAST) as g:
                body(g, False)
            body(LAST, True)

        @block.vector
        def _(dve):
            dve.sem_inc(bl_done, 2)
            dve.sem_inc(y_done, NT)
            dve.wait_ge(env["scales_in"], 32)

            def split(g):
                for c in range(0, HC, 2):
                    dve.wait_ge(ah_done, HC // 2 * g + c // 2 + 1)
                    nc.vector.tensor_tensor(al[:, c:c + 2, :], hin[:, c:c + 2, :], ah[:, c:c + 2, :].bitcast(F32), ALU.subtract).then_inc(al_done, 1)

            def body(g, last_block, first=False):
                for o in range(HC):
                    if first:
                        piece_lo(nc, dve, pieces, stage, o + 1, w_hi_done, w_lo_done)
                    dve.wait_ge(bh_done, HC * g + o + 1)
                    nc.vector.tensor_tensor(bl[:, o, :], hf[o % 2][:, :], bh[:, o, :].bitcast(F32), ALU.subtract).then_inc(bl_done, 1)
                if first:
                    piece_lo(nc, dve, pieces, stage, HC + 1, w_hi_done, w_lo_done)
                if not last_block:
                    split(g + 1)
                for t in range(NT):
                    dve.wait_ge(y_ps, NT * g + t + 1)
                    nc.vector.tensor_tensor(y[:, t, :], ps_y[t][:, 0:D], s3[:, :], ALU.mult).then_inc(y_done, 1)
                dve.wait_ge(y_done, NT * g + 2 * NT)
                layernorm_stats(nc, dve, lambda t: y[:, t, :], st, mv, stats, STATS * g)
                dve.wait_ge(rstd, 2 * g + 2)
                if not first:
                    dve.wait_ge(out_done, 16 * g)
                dve.wait_ge(x_in, 16 * g + 16)
                parts = 2 if last_block else 1
                for k in range(parts):
                    tiles = range(k * NT // parts, (k + 1) * NT // parts)
                    for t in tiles:
                        last = nc.vector.tensor_scalar(yo[:, t, :], y[:, t, :], mv[:, t, 0:1], rs[:, t:t + 1], ALU.subtract, ALU.mult)
                    last.then_inc(n_done, 1)
                    dve.wait_ge(n_done, g + k + 1)
                    part = slice(tiles[0], tiles[-1] + 1)
                    nc.vector.tensor_tensor(yo[:, part, :], yo[:, part, :], xr[:, part, :], ALU.add).then_inc(o_done, 1)

            piece_lo(nc, dve, pieces, stage, 0, w_hi_done, w_lo_done)
            split(0)
            body(0, False, first=True)
            with dve.Fori(1, LAST) as g:
                body(g, False)
            body(LAST, True)

        @block.tensor
        def _(pe):
            def body(g, exact):
                for o in range(HC):
                    pe.wait_ge(w_lo_done, o + 1)
                    pe.wait_ge(gelu_done, HC * g + o + 1)
                    dense_512(nc, ps_3[o % 4][:, :], h2h, h2l, ah, al, HC, o, exact,
                              ready=(lambda c: pe.wait_ge(al_done, HC // 2 * g + c // 2 + 1)) if o == 0 else None).then_inc(l3_ps, 1)
                pe.wait_ge(w_lo_done, len(pieces))
                pairs = passes(w3h, w3l, bh, bl, exact)
                for t in range(NT):
                    pe.wait_ge(y_done, NT * g + t + 1)
                    n = 0
                    for c in range(HC):
                        if t == 0:
                            pe.wait_ge(bl_done, HC * g + c + 3)
                        for w, a in pairs:
                            last = nc.tensor.matmul(ps_y[t][:, 0:D], a[:, c, t * P:(t + 1) * P], w[:, c, :],
                                                    start=(n == 0), stop=(n == len(pairs) * HC - 1))
                            n += 1
                    last.then_inc(y_ps, 1)

            def blocks(exact):
                with pe.Fori(0, BLOCKS) as g:
                    body(g, exact)

            by_weights(pe, env, blocks)


def build(nc, x, w_kqv, m, w1, w2, h1, h2w, w3, scales, s3, consts_in, ramp_in, out):
    env = dict(x=x, w_kqv=w_kqv, m=m, w1=w1, w2=w2, h1=h1, h2w=h2w, w3=w3, scales=scales, s3=s3, out=out,
               consts_in=consts_in, ramp_in=ramp_in)
    env["kst"] = nc.dram_tensor("kst", [B * H, 2 * HD, S], F32).ap()
    env["qst"] = nc.dram_tensor("qst", [B * H, 2 * HD + 2 * QB, S], F32).ap()
    env["vs"] = nc.dram_tensor("vs", [GROUPS, QB, P, NT, GH * VW], F32).ap()
    env["x1"] = nc.dram_tensor("x1", [BLOCKS, P, NT, D], F32).ap()
    env["h2"] = nc.dram_tensor("h2", [BLOCKS, P, HC, TB], F32).ap()
    with (
        nc.sbuf_tensor("consts", [P, 3 * P + 8], F32) as consts,
        nc.sbuf_tensor("ident_b", [P, P], BF16) as ident_b,
        nc.sbuf_tensor("mask_kq", [P, P], BF16) as mask_kq,
        nc.sbuf_tensor("mask_qk", [P, P], BF16) as mask_qk,
        nc.sbuf_tensor("neg_half", [P, NT], F32) as neg_half,
        nc.sbuf_tensor("eps", [P, NT], F32) as eps,
        nc.sbuf_tensor("inexact", [P, 1], F32) as inexact,
    ):
        env.update(consts=consts, ident_b=ident_b, mask_kq=mask_kq, mask_qk=mask_qk, neg_half=neg_half, eps=eps, inexact=inexact)
        with nc.sbuf_tensor("att", [P, BLOCKS * NT, D], F32) as att, ExitStack() as outer:
            env["att"] = att

            def sb(name, shape, dt=F32):
                return outer.enter_context(nc.sbuf_tensor(name, shape, dt))

            for name in ("xs", "xo", "xn"):
                env[name] = sb(name, [P, NT, D])
            env["raw"] = [sb(f"raw{n}", [P, NT, W_PIECE // NT]) for n in range(2)]
            env.update(st=sb("st", [P, NT, 6]), mv=sb("mv", [P, NT, 2]), tmp=sb("tmp", [P, NT]), rs=sb("rs", [P, NT]))
            for name in ("x_in", "stats", "rstd", "a_done", "x1_done", "xn_done", "x1_out"):
                env[name] = outer.enter_context(nc.semaphore(f"ln_{name}"))
            env["scales_sb"], env["s3_sb"] = sb("scales_sb", [P, 4, HC]), sb("s3_sb", [P, D])
            env["hin"] = att[:, 0:HC * TB // D, :].rearrange("p (c a) d -> p c (a d)", c=HC)
            for name in ("scales_in", "h_first"):
                env[name] = outer.enter_context(nc.semaphore(name))
            env["w2_in"] = [outer.enter_context(nc.semaphore(f"raw2_in{n}")) for n in range(2)]
            env["w_in"] = [outer.enter_context(nc.semaphore(f"raw_in{n}")) for n in range(2)]
            with ExitStack() as ctx:
                env["ramp_r"] = ctx.enter_context(nc.sbuf_tensor("ramp_r", [2 * QB + 2, S], F32R))
                for name in ("ks", "qs"):
                    env[name] = [[ctx.enter_context(nc.sbuf_tensor(f"{name}0{p}", [P, S], F32R)) for p in range(2)]]
                env["vg"] = [ctx.enter_context(nc.sbuf_tensor("vg0", [P, ST * GH * VW + OW - VW], F32))]
                for name in ("loaded", "ramp_set", "stored"):
                    env[name] = [ctx.enter_context(nc.semaphore(f"{name}{u}")) for u in range(2)]
                stage_projections(nc, env)
                stage_attention(nc, env)
            stage_ffn_in(nc, env)
            stage_ffn_out(nc, env)


def kernel(**inputs):
    import numpy as np
    import concourse.bacc as bacc
    from concourse import mybir as _mybir
    from concourse.bass_utils import run_bass_kernel_spmd

    get = {k.removeprefix("L0_"): np.asarray(v) for k, v in inputs.items()}
    consts = np.zeros((P, 3 * P + 8), np.float32)
    consts[:, 0:P] = np.eye(P)
    consts[:, P:2 * P] = np.tril(np.full((P, P), MASK), -1)
    consts[:, 2 * P:3 * P] = np.triu(np.full((P, P), MASK), 1)
    consts[:, 3 * P:] = np.tile(np.eye(8), (P // 8, 1))
    ramp = np.ones((2 * QB + 2, S), np.float32)
    for i in range(QB):
        ramp[i] = ramp[QB + i] = np.arange(S) - (TB * i + TB // 2)
    turned = {k: np.ascontiguousarray(get[f"ffn_{k}_w"].T) for k in ("w1", "w2", "h1", "h2", "w3")}
    scales = np.stack([get[f"ffn_{k}_s"].reshape(HC, P).T for k in ("w1", "w2", "h1", "h2")], 1)
    arrays = dict(x=get["attn_x"], w_kqv=get["attn_W_kqv"], m=get["attn_m"], w1=turned["w1"], w2=turned["w2"], h1=turned["h1"],
                  h2w=turned["h2"], w3=turned["w3"], scales=scales, s3=get["ffn_w3_s"], consts_in=consts, ramp_in=ramp)
    arrays = {f"in_{k}": np.ascontiguousarray(v) for k, v in arrays.items()}
    nc = bacc.Bacc("TRN2", target_bir_lowering=False, num_devices=1)
    args = [nc.dram_tensor(k, v.shape, _mybir.dt.from_np(v.dtype), kind="ExternalInput").ap() for k, v in arrays.items()]
    args.append(nc.dram_tensor("out_0", (B, S, D), F32, kind="ExternalOutput").ap())
    build(nc, *args)
    return run_bass_kernel_spmd(nc, [arrays], core_ids=[0]).results[0]["out_0"]
```
